# Optimizing a Trainium2 kernel written in Bass

```python
import numpy as np
import jax
import jax.numpy as jnp

def _softmax(x, axis=-1):
    return jax.nn.softmax(x, axis=axis)

def _gelu(x):
    return jax.nn.gelu(x, approximate=True)

def _silu(x):
    return jax.nn.silu(x)

def _sigmoid(x):
    return jax.nn.sigmoid(x)

def _layernorm(x, axis=-1, eps=1e-05):
    m = jnp.mean(x, axis=axis, keepdims=True)
    v = jnp.var(x, axis=axis, keepdims=True)
    return (x - m) / jnp.sqrt(v + eps)

def _scatter_add(tgt, idx, src, axis=0):
    return tgt.at[idx].add(src)

def _segment_sum(src, seg, n):
    return jax.ops.segment_sum(src, seg, n)
kernel_name = 'mk_gnn_preln_d2_gnn_r8_8e2f78'

def setup_inputs(seed: int=0):
    np.random.seed(seed)
    _w = jnp.asarray

    def _rec_inputs():
        import jax
        import jax.numpy as jnp
        _gk = jax.random.key(seed)
        x = -0.0003713 + 1 * jax.random.normal(jax.random.fold_in(_gk, 1), (6250, 256), jnp.float32)
        _s = jax.random.randint(jax.random.fold_in(_gk, 2), (50000,), 0, 6250, jnp.int32)
        _d = jax.random.randint(jax.random.fold_in(_gk, 3), (50000,), 0, 6250, jnp.int32)
        _loop = jnp.arange(6250, dtype=jnp.int32)
        src = jnp.concatenate([_s, _d, _loop])
        dst = jnp.concatenate([_d, _s, _loop])
        _o = jnp.argsort(dst, stable=True)
        src = src[_o]
        dst = dst[_o]
        edge_weight = jax.random.uniform(jax.random.fold_in(_gk, 13), (106250,), jnp.float32, 0.0, 1)
        return (x, src, dst, edge_weight)
    x, src, dst, edge_weight = _rec_inputs()

    def _L0_gnn_setup():
        import jax, jax.numpy as jnp
        import numpy as np
        N_NODES = 6250
        N_EDGES = 100000
        D_IN = 256
        D_HID = 256
        D_OUT = 256
        EPS = 1e-12

        def _sage_conv(x, src, dst, W_proj, b_proj, W_l, b_l, W_r):
            n = x.shape[0]
            xp = jax.nn.relu(x @ W_proj + b_proj)
            msg_sum = jax.ops.segment_sum(xp[src], dst, num_segments=n)
            cnt = jax.ops.segment_sum(jnp.ones_like(dst, dtype=x.dtype), dst, num_segments=n)
            aggr = msg_sum / jnp.maximum(cnt, 1.0)[:, None]
            out = aggr @ W_l + b_l + x @ W_r
            norm = jnp.linalg.norm(out, axis=-1, keepdims=True)
            return out / jnp.maximum(norm, EPS)
        key = jax.random.key(seed)
        ks = jax.random.split(key, 12)
        s = 1.0 / np.sqrt(D_IN)
        sh = 1.0 / np.sqrt(D_HID)
        inp = {'node_emb': jax.random.normal(ks[0], (N_NODES, D_IN), dtype=jnp.float32), 'edge_index': jax.random.randint(ks[1], (2, N_EDGES), 0, N_NODES, dtype=jnp.int64), 'W_proj1': jax.random.uniform(ks[2], (D_IN, D_IN), jnp.float32, -s, s), 'b_proj1': jax.random.uniform(ks[3], (D_IN,), jnp.float32, -s, s), 'W_l1': jax.random.uniform(ks[4], (D_IN, D_HID), jnp.float32, -s, s), 'b_l1': jax.random.uniform(ks[5], (D_HID,), jnp.float32, -s, s), 'W_r1': jax.random.uniform(ks[6], (D_IN, D_HID), jnp.float32, -s, s), 'W_proj2': jax.random.uniform(ks[7], (D_HID, D_HID), jnp.float32, -sh, sh), 'b_proj2': jax.random.uniform(ks[8], (D_HID,), jnp.float32, -sh, sh), 'W_l2': jax.random.uniform(ks[9], (D_HID, D_OUT), jnp.float32, -sh, sh), 'b_l2': jax.random.uniform(ks[10], (D_OUT,), jnp.float32, -sh, sh), 'W_r2': jax.random.uniform(ks[11], (D_HID, D_OUT), jnp.float32, -sh, sh)}
        return inp
    _L0_gnn_all = _L0_gnn_setup()
    _L0_gnn_in = {k: v for k, v in _L0_gnn_all.items() if k in ('W_proj1', 'b_proj1', 'W_l1', 'b_l1', 'W_r1', 'W_proj2', 'b_proj2', 'W_l2', 'b_l2', 'W_r2')}
    del _L0_gnn_all

    def _L1_gnn_setup():
        import jax, jax.numpy as jnp
        import numpy as np
        N_NODES = 6250
        N_EDGES = 100000
        F_IN = 256
        F_OUT = 64
        HEADS = 4
        LEAKY_ALPHA = 0.2
        key = jax.random.key(seed)
        ks = jax.random.split(key, 8)
        x = jax.random.normal(ks[0], (N_NODES, F_IN), dtype=jnp.float32)
        W = jax.random.normal(ks[1], (HEADS, F_IN, F_OUT), dtype=jnp.float32) * 0.05
        a_self = jax.random.normal(ks[2], (HEADS, F_OUT), dtype=jnp.float32) * 0.05
        a_neigh = jax.random.normal(ks[3], (HEADS, F_OUT), dtype=jnp.float32) * 0.05
        bias = jnp.zeros((HEADS, F_OUT), dtype=jnp.float32)
        adj_val = jnp.ones((N_EDGES,), dtype=jnp.float32)
        edge_row = jax.random.randint(ks[4], (N_EDGES,), 0, N_NODES, dtype=jnp.int32)
        edge_col = jax.random.randint(ks[5], (N_EDGES,), 0, N_NODES, dtype=jnp.int32)
        return {'x': x, 'W': W, 'a_self': a_self, 'a_neigh': a_neigh, 'bias': bias, 'adj_val': adj_val, 'edge_row': edge_row, 'edge_col': edge_col}
    _L1_gnn_all = _L1_gnn_setup()
    _L1_gnn_in = {k: v for k, v in _L1_gnn_all.items() if k in ('W', 'a_self', 'a_neigh', 'bias')}
    del _L1_gnn_all
    return {'x': x, 'src': src, 'dst': dst, 'edge_weight': edge_weight, 'L0_gnn_W_proj1': _L0_gnn_in['W_proj1'], 'L0_gnn_b_proj1': _L0_gnn_in['b_proj1'], 'L0_gnn_W_l1': _L0_gnn_in['W_l1'], 'L0_gnn_b_l1': _L0_gnn_in['b_l1'], 'L0_gnn_W_r1': _L0_gnn_in['W_r1'], 'L0_gnn_W_proj2': _L0_gnn_in['W_proj2'], 'L0_gnn_b_proj2': _L0_gnn_in['b_proj2'], 'L0_gnn_W_l2': _L0_gnn_in['W_l2'], 'L0_gnn_b_l2': _L0_gnn_in['b_l2'], 'L0_gnn_W_r2': _L0_gnn_in['W_r2'], 'L1_gnn_W': _L1_gnn_in['W'], 'L1_gnn_a_self': _L1_gnn_in['a_self'], 'L1_gnn_a_neigh': _L1_gnn_in['a_neigh'], 'L1_gnn_bias': _L1_gnn_in['bias']}

def reference(x, src, dst, edge_weight, L0_gnn_W_proj1, L0_gnn_b_proj1, L0_gnn_W_l1, L0_gnn_b_l1, L0_gnn_W_r1, L0_gnn_W_proj2, L0_gnn_b_proj2, L0_gnn_W_l2, L0_gnn_b_l2, L0_gnn_W_r2, L1_gnn_W, L1_gnn_a_self, L1_gnn_a_neigh, L1_gnn_bias):
    import jax
    import jax.numpy as jnp

    def _L0_gnn_ref(node_emb, edge_index, W_proj1, b_proj1, W_l1, b_l1, W_r1, W_proj2, b_proj2, W_l2, b_l2, W_r2):
        import jax, jax.numpy as jnp
        import numpy as np
        N_NODES = 6250
        N_EDGES = 100000
        D_IN = 256
        D_HID = 256
        D_OUT = 256
        EPS = 1e-12

        def _sage_conv(x, src, dst, W_proj, b_proj, W_l, b_l, W_r):
            n = x.shape[0]
            xp = jax.nn.relu(x @ W_proj + b_proj)
            msg_sum = jax.ops.segment_sum(xp[src], dst, num_segments=n)
            cnt = jax.ops.segment_sum(jnp.ones_like(dst, dtype=x.dtype), dst, num_segments=n)
            aggr = msg_sum / jnp.maximum(cnt, 1.0)[:, None]
            out = aggr @ W_l + b_l + x @ W_r
            norm = jnp.linalg.norm(out, axis=-1, keepdims=True)
            return out / jnp.maximum(norm, EPS)
        src, dst = (edge_index[0], edge_index[1])
        h = _sage_conv(node_emb, src, dst, W_proj1, b_proj1, W_l1, b_l1, W_r1)
        h = jax.nn.relu(h)
        out = _sage_conv(h, src, dst, W_proj2, b_proj2, W_l2, b_l2, W_r2)
        return out

    def _L1_gnn_ref(x, W, a_self, a_neigh, bias, adj_val, edge_row, edge_col):
        import jax, jax.numpy as jnp
        import numpy as np
        N_NODES = 6250
        N_EDGES = 100000
        F_IN = 256
        F_OUT = 64
        HEADS = 4
        LEAKY_ALPHA = 0.2
        N = x.shape[0]
        feats = jnp.einsum('nf,hfo->hno', x, W)
        s_self = jnp.einsum('hno,ho->hn', feats, a_self)
        s_neigh = jnp.einsum('hno,ho->hn', feats, a_neigh)
        z = s_self[:, edge_row] + s_neigh[:, edge_col]
        e = jnp.where(z > 0, z, LEAKY_ALPHA * z) * adj_val[None, :]

        def seg_softmax(e_h):
            m = jax.ops.segment_max(e_h, edge_row, num_segments=N)
            ex = jnp.exp(e_h - m[edge_row])
            s = jax.ops.segment_sum(ex, edge_row, num_segments=N)
            return ex / s[edge_row]
        alpha = jax.vmap(seg_softmax)(e)

        def aggregate(alpha_h, feat_h):
            return jax.ops.segment_sum(alpha_h[:, None] * feat_h[edge_col], edge_row, num_segments=N)
        out = jax.vmap(aggregate)(alpha, feats) + bias[:, None, :]
        out = jnp.transpose(out, (1, 0, 2)).reshape(N, -1)
        return jax.nn.relu(out)
    edge_index = jnp.stack([src, dst])
    h = jnp.maximum(_layernorm(x, axis=-1), 0.0)
    x = x + _L0_gnn_ref(h, edge_index, L0_gnn_W_proj1, L0_gnn_b_proj1, L0_gnn_W_l1, L0_gnn_b_l1, L0_gnn_W_r1, L0_gnn_W_proj2, L0_gnn_b_proj2, L0_gnn_W_l2, L0_gnn_b_l2, L0_gnn_W_r2)
    h = jnp.maximum(_layernorm(x, axis=-1), 0.0)
    x = x + _L1_gnn_ref(h, L1_gnn_W, L1_gnn_a_self, L1_gnn_a_neigh, L1_gnn_bias, edge_weight, src, dst)
    return x

_drawn_inputs = setup_inputs


def setup_inputs(seed=0):
    import zlib

    import numpy as np

    out = dict(_drawn_inputs(seed))
    spreads = {'L1_gnn_bias': (0.0, 0.1)}
    factors = {'edge_weight': 8.0,
     'L0_gnn_W_proj1': 8.0,
     'L0_gnn_b_proj1': 64.0,
     'L0_gnn_W_l1': 6.128,
     'L0_gnn_b_l1': 64.0,
     'L0_gnn_W_proj2': 5.75,
     'L0_gnn_b_proj2': 3.563,
     'L1_gnn_a_self': 8.0,
     'L1_gnn_a_neigh': 8.0,
     'L0_gnn_W_r1': 8.0,
     'L0_gnn_W_r2': 2.803}
    for name, (base, spread) in spreads.items():
        noise = np.random.default_rng([zlib.crc32(name.encode()), seed]).standard_normal(out[name].shape)
        drawn = base * np.exp(spread * noise) if base else spread * noise
        out[name] = jnp.asarray(drawn.astype(out[name].dtype))
    for name, factor in factors.items():
        out[name] = (out[name] * factor).astype(out[name].dtype)
    return out
```

```python
import concourse.bass as bass
from concourse import mybir

NODES, D, EDGES = 6250, 256, 106250
P = 128
HEADS, HD = 4, 64
TILES = -(-NODES // P)
ROWS = 52 * P

CHUNKS = 13
GE = P * CHUNKS
GROUPS = -(-EDGES // GE)
ALL = GROUPS * CHUNKS
SPARE_T = min(t for t in range(1, 53) if (ROWS - NODES) % t == 0 and (ROWS - NODES) // t <= P)
SPARE_P = (ROWS - NODES) // SPARE_T
NO_NODE = 1 << 20

BLOCKS = 26
BC = ALL // 2 // BLOCKS
HALF_EDGES = ALL // 2 * P
PAD_SRC = TILES * P
ACHUNKS = 18
AE = P * ACHUNKS
MOST = EDGES // AE + TILES
RING = 3
ASTEPS = -(-MOST // RING) * RING + RING + 1
NEG = -1.0e30
PART = 6
PQ = PART * HEADS
BY_DVE = 5
GW = 264
EPS_LN, EPS_NORM = 1e-5, 1e-12


def gnn_program(nc, x, src_g, dst_g, dst_s, src_p, src_b, dst_b, w_b, Wp1, bp1, Wl1, bl1, Wr1, Wp2, bp2, Wl2, bl2,
                Wr2, W, a_self, a_neigh, bias, out):
    f32, bf16, i32 = mybir.dt.float32, mybir.dt.bfloat16, mybir.dt.int32
    ALU, ACT, AX = mybir.AluOpType, mybir.ActivationFunctionType, mybir.AxisListType

    def sb(name, shape, dt=f32):
        return nc.alloc_sbuf_tensor(name, shape, dt)

    def table(name, width):
        return nc.dram_tensor(name, [ROWS, width], f32).ap()

    def semaphores(tag, single, rings=(), size=2):
        made = {n: nc.alloc_semaphore(f"{tag}_{n}") for n in single}
        made.update({n: [nc.alloc_semaphore(f"{tag}_{n}{j}") for j in range(size)] for n in rings})
        return made

    def finish(S):
        for sem in S.values():
            for one in (sem if isinstance(sem, list) else [sem]):
                nc.sync.sem_clear(one)
                nc.release_semaphore(one)
        nc.all_engine_barrier()

    G1 = semaphores("gather1", [], ["rows"])
    G2 = semaphores("gather2", [], ["rows"])
    G3 = semaphores("gather3", [], ["rows"], RING)
    GS = semaphores("scatter", [], ["records"])
    passed = {e.engine: nc.alloc_semaphore(f"passed_{n}") for n, e in
              (("act", nc.scalar), ("dve", nc.vector), ("pool", nc.gpsimd), ("sp", nc.sync))}

    def wait_here(e, sem, value):
        e.wait_ge(sem, value)
        e.sem_inc(passed[e.engine], 1)

    msg1, msg2 = table("msg1", D), table("msg2", D)
    msg3 = table("msg3", D + HEADS)
    sum1, sum2 = table("sum1", D + 1), table("sum2", D + 1)
    root1, root2 = table("root1", D), table("root2", D)
    x1 = table("x1", D)
    self3 = table("self3", HEADS)
    att3 = table("att3", D + 2 * HEADS)
    tile_d = nc.dram_tensor("tile_d", [2, HALF_EDGES + 2 * BC * P], bf16).ap()
    rec_d = nc.dram_tensor("rec_d", [ASTEPS * AE, 4], i32).ap()

    ident = sb("ident", [P, P])
    identb = sb("identb", [P, P], bf16)
    negid = sb("negid", [P, P], bf16)
    iota_i = sb("iota_i", [P, P], i32)
    iota_row = sb("iota_row", [P, P])
    ones = sb("ones", [P, P])
    sel = sb("sel", [3 * PQ, PQ, P], bf16)
    base0_t, base_t = sb("base0_t", [P, GROUPS]), sb("base_t", [P, GROUPS])
    base_i = sb("base_i", [1, GROUPS], i32)
    pairs_i = sb("pairs_i", [1, 1], i32)
    base3_t, base3_i = sb("base3_t", [P, ASTEPS]), sb("base3_i", [1, ASTEPS], i32)
    rounds_i = sb("rounds_i", [1, 1], i32)
    wl1, wl2 = sb("wl1", [P, 2, D]), sb("wl2", [P, 2, D])
    wpr1, wpr2 = sb("wpr1", [P, 2, 2 * D]), sb("wpr2", [P, 2, 2 * D])
    b1, b2 = sb("b1", [P, 2 * D]), sb("b2", [P, 2 * D])
    wg = sb("wg", [P, 2, D + 2 * HEADS])
    bias_t = sb("bias_t", [P, D])

    G = sb("G", [P, RING, ACHUNKS, GW])
    OH = sb("OH", [P, RING, ACHUNKS, P])
    idx = sb("idx", [P, 2, CHUNKS], i32)
    dst = sb("dst", [P, 2, CHUNKS], i32)
    dstrel = sb("dstrel", [P, RING, ACHUNKS])
    old = sb("old", [P, RING, D + 2 * HEADS])
    root = sb("root", [P, 2, D])
    xw = sb("xw", [P, RING, D])
    new = sb("new", [P, D + 2 * HEADS])
    cnt = sb("cnt", [P, 2])
    aggr = sb("aggr", [P, D])
    aT = sb("aT", [P, 2, P])
    o = sb("o", [P, D])
    junk = sb("junk", [P, D])
    nrm = sb("nrm", [P, 4])
    stats, mv, rs = sb("stats", [P, 6]), sb("mv", [P, 2]), sb("rs", [P, 4])
    h = sb("h", [P, D])
    hT = sb("hT", [P, 2, P])
    y = sb("y", [P, 2 * D])
    x1n = sb("x1n", [P, D])
    V = sb("V", [P, ACHUNKS, D + HEADS])
    Vflat = V[:, :, :].rearrange("p k w -> p (k w)")
    psum = [nc.alloc_psum_tensor(f"bank{i}", [P, 512], f32) for i in range(8)]
    tpA, tpH, po, py = psum[2], psum[3], psum[4], psum[5]

    S0 = semaphores("prep", ["w", "ident", "iota", "const", "dsts", "srcs", "ready", "mm", "chain", "diag", "zero", "zeroed",
                             "tri", "tiles", "counted", "counts", "groups", "starts", "cmp", "bases"])
    n_of = {}
    dsts = OH[:, 0, :, :].rearrange("p k n -> p (k n)").bitcast(i32)[0:GROUPS, 0:GE]
    srcs, tile_i = Vflat[:, 0:ALL].bitcast(i32), Vflat[:, ALL:2 * ALL].bitcast(i32)
    tile_b = sb("tile_b", [P, ALL], bf16)
    equal_b = sb("equal_b", [P, ALL], bf16)
    mm_f = sb("mm_f", [GROUPS, 2])
    dg = sb("dg", [GROUPS, 2, GROUPS])
    bt = sb("bt", [P, 4, GROUPS])
    flag = sb("flag", [P, 2])
    abc = sb("abc", [P, 2, D])
    counts = sb("counts", [P, P])
    tri = sb("tri", [P, P])
    before49 = sb("before49", [P, P])
    halves = sb("halves", [P, 2])
    cnt2 = sb("cnt2", [P, 4])
    ngroups = sb("ngroups", [P, 4])
    cmp = sb("cmp", [P, ASTEPS])
    rnd = sb("rnd", [P, 4])
    scan0 = sb("scan0", [P, 1])
    part_i, part_f, tile_p = sb("part_i", [P, 1], i32), sb("part_f", [P, 1]), sb("tile_p", [P, 1])
    sizes_t = sb("sizes_t", [P, ASTEPS])
    Gflat = G[:, :, :, :].rearrange("p a k w -> p (a k w)")
    zrow = Gflat[:, 0:(ROWS // P) * GW].rearrange("p (t w) -> p t w", w=GW)
    empty = OH[:, 1:3, :, :].rearrange("p a k n -> p (a k n)").bitcast(i32)
    with nc.Block() as block:
        @block.sync
        def _(sp):
            sp.dma_start(srcs[:, :], src_p).then_inc(S0["srcs"], 16)
            sp.dma_start(dsts, dst_s).then_inc(S0["dsts"], 16)
            n = 0
            for c in range(2):
                rows = slice(c * P, (c + 1) * P)
                for to, of in ((wl1[:, c, :], Wl1[rows, :]), (wl2[:, c, :], Wl2[rows, :]),
                               (wpr1[:, c, 0:D], Wp1[rows, :]), (wpr1[:, c, D:2 * D], Wr1[rows, :]),
                               (wpr2[:, c, 0:D], Wp2[rows, :]), (wpr2[:, c, D:2 * D], Wr2[rows, :]),
                               (wg[:, c, 0:D].rearrange("p (h o) -> p h o", h=HEADS),
                                W[:, rows, :].rearrange("h p o -> p h o"))):
                    sp.dma_start(to, of).then_inc(S0["w"], 16)
                    n += 1
            for to, of in ((b1[:, 0:D], bp1), (b1[:, D:2 * D], bl1), (b2[:, 0:D], bp2), (b2[:, D:2 * D], bl2),
                           (abc[:, 0, :], a_neigh), (abc[:, 1, :], a_self), (bias_t[:, :], bias)):
                sp.dma_start(to, of.rearrange("(a n) -> a n", a=1).to_broadcast([P, D])).then_inc(S0["w"], 16)
                n += 1
            n_of["weights"] = n
            sp.wait_ge(S0["tiles"], 1)
            for half in range(2):
                sp.dma_start(tile_d[half, 0:HALF_EDGES].rearrange("(p n) -> p n", p=P // 2),
                             tile_b[half * (P // 2):(half + 1) * (P // 2), :]).then_inc(S0["zeroed"], 16)
            sp.wait_ge(S0["zero"], 4)
            sp.dma_start(tile_d[:, HALF_EDGES:], Gflat[0:2, 0:BC * P].bitcast(bf16)).then_inc(S0["zeroed"], 16)
            sp.dma_start(att3.rearrange("(p t) d -> p t d", p=P), zrow).then_inc(S0["zeroed"], 16)
            for t in (sum1, sum2):
                sp.dma_start(t.rearrange("(p t) d -> p t d", p=P), zrow[:, :, 0:D + 1]).then_inc(S0["zeroed"], 16)
            for t, width in ((x1, D), (self3, HEADS)):
                sp.dma_start(t[NODES:, :].rearrange("(t p) d -> p t d", t=SPARE_T),
                             zrow[0:SPARE_P, 0:SPARE_T, 0:width]).then_inc(S0["zeroed"], 16)
            rec_w = rec_d.rearrange("(p n) c -> p (n c)", p=P)
            at, width, pieces = 0, ASTEPS * AE * 4 // P, 0
            while at < width:
                m = min(empty.shape[1], width - at)
                sp.dma_start(rec_w[:, at:at + m], empty[:, 0:m]).then_inc(S0["zeroed"], 16)
                at, pieces = at + m, pieces + 1
            n_of["zeroed"] = 8 + pieces
            sp.wait_ge(S0["zeroed"], 16 * n_of["zeroed"])
            sp.wait_ge(S0["w"], 16 * n)

        @block.gpsimd
        def _(pool):
            pool.memset(ident[:, :], 0.0).then_inc(S0["ident"], 1)
            pool.wait_ge(S0["ident"], 1)
            pool.affine_select(out=ident[:, :], in_=ident[:, :], compare_op=ALU.not_equal, fill=1.0, base=0,
                               pattern=[[-1, P]], channel_multiplier=1).then_inc(S0["ident"], 1)
            pool.iota(iota_i[:, :], [[1, P]], base=0, channel_multiplier=0).then_inc(S0["iota"], 1)
            pool.iota(part_i[:, :], [[0, 1]], base=0, channel_multiplier=1).then_inc(S0["iota"], 1)
            pool.memset(tri[:, :], 1.0).then_inc(S0["tri"], 1)
            pool.memset(before49[:, :], 1.0).then_inc(S0["tri"], 1)
            pool.memset(halves[:, :], 1.0).then_inc(S0["tri"], 1)
            pool.wait_ge(S0["tri"], 3)
            pool.affine_select(out=tri[:, :].rearrange("p (a m) -> p a m", a=2),
                               in_=tri[:, :].rearrange("p (a m) -> p a m", a=2), compare_op=ALU.is_ge, fill=0.0,
                               base=-1, pattern=[[0, 2], [1, P // 2]], channel_multiplier=-1).then_inc(S0["tri"], 1)
            pool.affine_select(out=before49[:, :], in_=before49[:, :], compare_op=ALU.is_ge, fill=0.0,
                               base=TILES - 1, pattern=[[0, P]], channel_multiplier=-1).then_inc(S0["tri"], 1)
            pool.affine_select(out=halves[:, 0:1], in_=halves[:, 0:1], compare_op=ALU.is_ge, fill=0.0,
                               base=P // 2 - 1, pattern=[[0, 1]], channel_multiplier=-1).then_inc(S0["tri"], 1)
            pool.affine_select(out=halves[:, 1:2], in_=halves[:, 1:2], compare_op=ALU.is_ge, fill=0.0,
                               base=-P // 2, pattern=[[0, 1]], channel_multiplier=1).then_inc(S0["tri"], 1)
            pool.memset(sel[:, :, :], 0.0).then_inc(S0["const"], 1)
            for part in range(3):
                pool.wait_ge(S0["const"], part + 1)
                pool.affine_select(out=sel[:, :, :], in_=sel[:, :, :], compare_op=ALU.not_equal, fill=1.0,
                                   base=-part * PQ, pattern=[[-1, PQ], [0, P]],
                                   channel_multiplier=1).then_inc(S0["const"], 1)

        @block.vector
        def _(dve):
            chained = [0]

            def link(ins):
                chained[0] += 1
                ins.then_inc(S0["chain"], 1)
                dve.wait_ge(S0["chain"], chained[0])

            dve.wait_ge(S0["srcs"], 16)
            link(dve.tensor_scalar(tile_i[:, :], srcs[:, :], 7, None, ALU.logical_shift_right))
            link(dve.tensor_copy(tile_b[:, :], tile_i[:, :]))
            dve.sem_inc(S0["tiles"], 1)
            link(dve.memset(zrow[:, :, 0:D + HEADS], 0.0))
            link(dve.memset(zrow[:, :, D + HEADS:], NEG))
            link(dve.memset(empty, 0))
            link(dve.memset(empty.rearrange("p (n c) -> p n c", c=4)[:, :, 1:2], NO_NODE))
            dve.sem_inc(S0["zero"], 4)
            dve.memset(ones[:, :], 1.0).then_inc(S0["ready"], 1)
            link(dve.memset(counts[:, :], 0.0))
            for t in range(TILES + 1):
                link(dve.tensor_scalar(equal_b[:, :], tile_b[:, :], float(t), None, ALU.is_equal, ALU.add,
                                       accum_out=counts[:, t:t + 1]))
            link(dve.tensor_copy(counts[:, P // 2:P // 2 + TILES + 1], counts[:, 0:TILES + 1]))
            dve.sem_inc(S0["counted"], 1)
            dve.wait_ge(S0["ident"], 2)
            link(dve.tensor_copy(identb[:, :], ident[:, :]))
            link(dve.tensor_scalar(negid[:, :], ident[:, :], NEG, None, ALU.mult))
            dve.wait_ge(S0["iota"], 2)
            link(dve.tensor_copy(iota_row[:, :], iota_i[:, :]))
            dve.wait_ge(S0["counts"], 1)
            link(dve.tensor_copy(cnt2[:, 0:2], psum[1][:, 0:2]))
            link(dve.tensor_tensor(cnt2[:, 2:3], cnt2[:, 0:1], cnt2[:, 1:2], ALU.add))
            link(dve.tensor_scalar(sizes_t[:, :], iota_row[:, 0:ASTEPS], float(AE), None, ALU.mult))
            link(dve.tensor_scalar(cmp[:, :], sizes_t[:, :], cnt2[:, 2:3], None, ALU.is_lt, ALU.add,
                                   accum_out=ngroups[:, 0:1]))
            link(dve.tensor_scalar(ngroups[:, 1:2], ngroups[:, 0:1], 1.0, None, ALU.max))
            dve.sem_inc(S0["groups"], 1)
            dve.wait_ge(S0["starts"], 1)
            link(dve.tensor_copy(rnd[:, 0:2], psum[2][:, 0:2]))
            dve.wait_ge(S0["tri"], 7)
            link(dve.tensor_copy(part_f[:, :], part_i[:, :]))
            link(dve.scalar_tensor_tensor(out=tile_p[:, :], in0=halves[:, 1:2], scalar=-float(P // 2), in1=part_f[:, :],
                                          op0=ALU.mult, op1=ALU.add))
            link(dve.tensor_tensor(rnd[:, 2:3], cnt2[:, 0:1], halves[:, 1:2], ALU.mult))
            link(dve.scalar_tensor_tensor(out=scan0[:, :], in0=rnd[:, 0:1], scalar=float(AE), in1=rnd[:, 2:3],
                                          op0=ALU.mult, op1=ALU.add))
            link(dve.tensor_scalar(cmp[:, :], iota_row[:, 0:ASTEPS], rnd[:, 0:1], None, ALU.is_ge))
            dve.sem_inc(S0["cmp"], 1)
            dve.wait_ge(S0["bases"], 1)
            link(dve.tensor_scalar(base3_t[:, :], psum[3][:, 0:ASTEPS], -1.0, float(P), ALU.add, ALU.mult))
            link(dve.tensor_copy(base3_i[:, :], base3_t[0:1, :]))
            link(dve.tensor_scalar(sizes_t[:, :], iota_row[:, 0:ASTEPS], float(RING), None, ALU.mult))
            link(dve.tensor_scalar(cmp[:, :], sizes_t[:, :], rnd[:, 1:2], None, ALU.is_lt, ALU.add,
                                   accum_out=rnd[:, 3:4]))
            link(dve.tensor_scalar(rounds_i[:, :], rnd[0:1, 3:4], -1.0, None, ALU.add))
            dve.wait_ge(S0["dsts"], 16)
            link(dve.tensor_reduce(mm_f[:, 0:1], dsts, axis=AX.X, op=ALU.min))
            link(dve.tensor_reduce(mm_f[:, 1:2], dsts, axis=AX.X, op=ALU.max))
            link(dve.tensor_scalar(mm_f[:, 1:2], mm_f[:, 1:2], float(NODES - 1), None, ALU.min))
            for k in range(2):
                dve.tensor_scalar(dg[:, k, :], ident[0:GROUPS, 0:GROUPS], mm_f[:, k:k + 1], None,
                                  ALU.mult).then_inc(S0["diag"], 1)
            dve.wait_ge(S0["mm"], 1)
            lo, hi = bt[:, 0, :], bt[:, 1, :]
            link(dve.tensor_copy(lo, psum[0][:, 0:GROUPS]))
            link(dve.tensor_copy(hi, psum[0][:, GROUPS:2 * GROUPS]))
            link(dve.tensor_tensor(bt[:, 2, :], hi, lo, ALU.subtract))
            link(dve.tensor_scalar(bt[:, 2, :], bt[:, 2, :], float(P - 1), None, ALU.is_le))
            link(dve.tensor_tensor(bt[:, 3, 0:GROUPS - 1], bt[:, 0, 1:GROUPS], bt[:, 0, 0:GROUPS - 1], ALU.subtract))
            link(dve.tensor_scalar(bt[:, 3, 0:GROUPS - 1], bt[:, 3, 0:GROUPS - 1], float(P), None, ALU.is_le))
            link(dve.tensor_scalar(bt[:, 3, GROUPS - 1:GROUPS], bt[:, 0, GROUPS - 1:GROUPS], float(NODES - P), None,
                                   ALU.is_ge))
            link(dve.tensor_tensor(bt[:, 2, :], bt[:, 2, :], bt[:, 3, :], ALU.mult))
            link(dve.tensor_scalar(bt[:, 3, 0:1], bt[:, 0, 0:1], 0.0, None, ALU.is_le))
            link(dve.tensor_tensor(bt[:, 2, 0:1], bt[:, 2, 0:1], bt[:, 3, 0:1], ALU.mult))
            link(dve.tensor_reduce(flag[:, 0:1], bt[:, 2, :], axis=AX.X, op=ALU.min))
            link(dve.tensor_scalar(flag[:, 1:2], flag[:, 0:1], float((1 - TILES) * (GROUPS // 2)),
                                   float(TILES * (GROUPS // 2) - 1), ALU.mult, ALU.add))
            link(dve.tensor_copy(pairs_i[:, :], flag[0:1, 1:2]))
            link(dve.tensor_scalar(base0_t[:, :], lo, flag[:, 0:1], None, ALU.mult))
            link(dve.tensor_copy(base_i[:, :], base0_t[0:1, :]))
            dve.wait_ge(S0["w"], 16 * n_of["weights"])
            for k in range(2):
                for c in range(2):
                    link(dve.tensor_tensor(junk[:, :], wg[:, c, 0:D], abc[:, k, :], ALU.mult))
                    link(dve.tensor_reduce(wg[:, c, D + k * HEADS:D + (k + 1) * HEADS],
                                           junk[:, :].rearrange("p (h o) -> p h o", h=HEADS), axis=AX.X, op=ALU.add))
            dve.wait_ge(S0["zeroed"], 16 * n_of["zeroed"])
            link(dve.memset(G[:, :, :, D:D + 1], 1.0))

        @block.tensor
        def _(pe):
            pe.wait_ge(S0["ready"], 1)
            pe.wait_ge(S0["tri"], 7)
            pe.wait_ge(S0["counted"], 1)
            pe.matmul(psum[1][:, 0:2], counts[:, :], halves[:, :], start=True, stop=True).then_inc(S0["counts"], 1)
            pe.wait_ge(S0["groups"], 1)
            pe.matmul(psum[2][:, 0:1], tri[:, :], ngroups[:, 1:2], start=True, stop=True)
            pe.matmul(psum[2][:, 1:2], before49[:, :], ngroups[:, 1:2], start=True, stop=True).then_inc(S0["starts"], 1)
            pe.wait_ge(S0["cmp"], 1)
            pe.matmul(psum[3][:, 0:ASTEPS], ones[0:TILES + 1, :], cmp[0:TILES + 1, :], start=True,
                      stop=True).then_inc(S0["bases"], 1)
            pe.wait_ge(S0["diag"], 2)
            pe.matmul(psum[0][:, 0:2 * GROUPS], ones[0:GROUPS, :], dg[:, :, :].rearrange("p a b -> p (a b)"),
                      start=True, stop=True).then_inc(S0["mm"], 1)
    finish(S0)

    def transpose_h(pe, S, done):
        pe.wait_ge(S["h"], done)
        for c in range(2):
            ins = pe.transpose(tpH[:, c * P:(c + 1) * P], h[:, c * P:(c + 1) * P], ident[:, :])
        ins.then_inc(S["h_transposed"], 1)

    def copy_hT(act, S, done):
        act.wait_ge(S["h_transposed"], done)
        act.copy(hT[:, :, :].rearrange("p c n -> p (c n)"), tpH[:, 0:D]).then_inc(S["hT"], 1)

    def project(pe, S, done, weights, width):
        pe.wait_ge(S["hT"], done)
        for c in range(2):
            ins = pe.matmul(py[:, 0:width], hT[:, c, :], weights[:, c, :], start=(c == 0), stop=(c == 1))
        ins.then_inc(S["projected"], 1)

    def layer_norm_dve(dve, S, done, rows):
        dve.bn_stats(stats[:, :], rows).then_inc(S["stats"], 1)
        wait_here(dve, S["stats"], done)
        dve.bn_aggr(mv[:, :], stats[:, :]).then_inc(S["mv"], 1)
        dve.wait_ge(S["mv"], done)
        dve.tensor_scalar(rs[:, 0:1], mv[:, 1:2], EPS_LN, None, ALU.add).then_inc(S["var"], 1)
        dve.wait_ge(S["std"], done)
        dve.reciprocal(rs[:, 2:3], rs[:, 1:2]).then_inc(S["rstd"], 1)
        dve.wait_ge(S["rstd"], done)
        dve.scalar_tensor_tensor(out=rs[:, 3:4], in0=mv[:, 0:1], scalar=-1.0, in1=rs[:, 2:3], op0=ALU.mult,
                                 op1=ALU.mult).then_inc(S["shift"], 1)

    def layer_norm_act(act, S, done, rows):
        act.wait_ge(S["var"], done)
        act.activation(rs[:, 1:2], rs[:, 0:1], ACT.Sqrt).then_inc(S["std"], 1)
        act.wait_ge(S["shift"], done)
        act.activation(h[:, :], rows, ACT.Relu, bias=rs[:, 3:4], scale=rs[:, 2:3]).then_inc(S["h"], 1)

    def add_bias(dve, S, done, b):
        dve.wait_ge(S["projected"], done)
        dve.tensor_tensor(y[:, :], py[:, :], b[:, :], ALU.add).then_inc(S["biased"], 1)

    def relu_and_store(act, S, done, msg, rt):
        act.wait_ge(S["biased"], done)
        act.activation(y[:, 0:D], y[:, 0:D], ACT.Relu).then_inc(S["y"], 1)
        act.wait_ge(S["y"], done)
        act.dma_start(msg, y[:, 0:D]).then_inc(S["stored"], 16)
        act.dma_start(rt, y[:, D:2 * D]).then_inc(S["stored"], 16)

    S1 = semaphores("first", ["stats", "mv", "var", "std", "rstd", "shift", "h", "h_transposed", "hT", "projected",
                              "biased", "y", "stored", "member", "running", "place", "places", "carried",
                              "start"], ["x", "tiles", "edges", "records", "place_i", "free"])
    BN = BC * P
    trow = sb("trow", [P, 2, BN], bf16)
    member = sb("member", [P, BN], bf16)
    zero_b = sb("zero_b", [P, BN], bf16)
    running, place = Vflat[:, 0:BN], Vflat[:, BN:2 * BN]
    place_i = sb("place_i", [P, 2, BC, 2], i32)
    edges_i = sb("edges_i", [P, 2, 3, 2 * BC], i32)
    rec = sb("rec", [P, 2, 2 * BC, 4], i32)
    pplace = psum[6]
    with nc.Block() as block:
        @block.sync
        def _(sp):
            def load_x(tile, j):
                sp.dma_start(xw[:, j, :], x[bass.ds(tile * P, P), :]).then_inc(S1["x"][j], 16)

            def load_edges(i, q):
                for half in range(2):
                    sp.dma_start(trow[half * (P // 2):(half + 1) * (P // 2), q, :],
                                 tile_d[half:half + 1, bass.ds(i * BN, BN)].to_broadcast([P // 2, BN])
                                 ).then_inc(S1["tiles"][q], 16)
                for n, of in enumerate((dst_b, src_b, w_b)):
                    to = edges_i[:, q, n, :]
                    sp.dma_start(to if n < 2 else to.bitcast(f32),
                                 of[bass.ds(i, 1), :, :].rearrange("a p k -> (a p) k")).then_inc(S1["edges"][q], 16)

            for j in range(2):
                sp.sem_inc(S1["free"][j], 1)
                load_x(j, j)
                load_edges(j, j)
            with sp.Fori(0, BLOCKS // 2) as i:
                for q in range(2):
                    tile = sp.snap(i * 4 + 2 * q)
                    block_next, rounds_done = sp.snap(i * 2 + (q + 2)), sp.snap(i + 1)
                    scattered = sp.snap(rounds_done * (2 * BC * 16))
                    for j in range(2):
                        tile_next = sp.snap(tile + (j + 2))
                        sp.wait_ge(S1["h"], tile + (j + 1))
                        load_x(tile_next, j)
                    wait_here(sp, S1["member"], i * 2 + (q + 1))
                    sp.wait_ge(S1["records"][q], rounds_done)
                    load_edges(block_next, q)
                    sp.wait_ge(GS["records"][q], scattered)
                    sp.sem_inc(S1["free"][q], 1)
            for j in range(2):
                sp.wait_ge(S1["x"][j], (BLOCKS + 1) * 16)
                sp.wait_ge(S1["tiles"][j], (BLOCKS // 2 + 1) * 32)
                sp.wait_ge(S1["edges"][j], (BLOCKS // 2 + 1) * 48)

        @block.gpsimd
        def _(pool):
            with pool.Fori(0, BLOCKS // 2) as i:
                for q in range(2):
                    wait_here(pool, S1["place_i"][q], i + 1)
                    wait_here(pool, S1["records"][q], i + 1)
                    for k in range(2 * BC):
                        pool.indirect_dma_start(
                            out=rec_d[:, :], out_offset=bass.IndirectOffsetOnAxis(
                                ap=place_i[:, q, k % BC, k // BC:k // BC + 1], axis=0),
                            in_=rec[:, q, k, :], in_offset=None).then_inc(GS["records"][q], 16)
            for q in range(2):
                wait_here(pool, GS["records"][q], BLOCKS // 2 * 2 * BC * 16)

        @block.vector
        def _(dve):
            dve.memset(zero_b[:, :], 0.0).then_inc(S1["start"], 1)
            dve.memset(rec[:, :, :, :], 0).then_inc(S1["start"], 1)
            dve.wait_ge(S1["start"], 2)

            def sort_block(i, q, d):
                dve.wait_ge(S1["tiles"][q], (i + 1) * 32)
                dve.tensor_scalar(member[:, :], trow[:, q, :], tile_p[:, 0:1], None, ALU.is_equal).then_inc(S1["member"], 1)
                dve.wait_ge(S1["member"], d)
                dve.tensor_tensor_scan(out=running[:, :], data0=member[:, :], data1=zero_b[:, :],
                                       initial=scan0[:, 0:1], op0=ALU.add, op1=ALU.add).then_inc(S1["running"], 1)
                dve.wait_ge(S1["running"], d)
                dve.scalar_tensor_tensor(out=place[:, :], in0=running[:, :], scalar=-1.0, in1=member[:, :],
                                         op0=ALU.add, op1=ALU.mult).then_inc(S1["place"], 1)
                dve.tensor_copy(scan0[:, :], running[:, BN - 1:BN]).then_inc(S1["carried"], 1)
                dve.wait_ge(S1["carried"], d)

            with dve.Fori(0, BLOCKS // 2) as i:
                for q in range(2):
                    d = dve.snap(i * 2 + (q + 1))
                    sort_block(i, q, d)
                    for j in range(2):
                        tile = dve.snap(i * 4 + (2 * q + j))
                        done = dve.snap(tile + 1)
                        dve.wait_ge(S1["x"][j], d * 16)
                        layer_norm_dve(dve, S1, done, xw[:, j, :])
                        if j == 0:
                            dve.wait_ge(S1["edges"][q], (i + 1) * 48)
                            dve.wait_ge(S1["free"][q], i + 1)
                            dve.wait_ge(S1["places"], d)
                            dve.tensor_copy(place_i[:, q, :, :].rearrange("p k a -> p (k a)"),
                                            pplace[:, 0:2 * BC]).then_inc(S1["place_i"][q], 1)
                            for n in range(3):
                                ins = dve.tensor_copy(rec[:, q, :, n], edges_i[:, q, n, :])
                            ins.then_inc(S1["records"][q], 1)
                        dve.wait_ge(S1["stored"], tile * 32 + 32)
                        add_bias(dve, S1, done, b1)

        @block.scalar
        def _(act):
            act.sem_inc(S1["stored"], 32)
            with act.Fori(0, BLOCKS) as i:
                for j in range(2):
                    done = act.snap(i * 2 + (j + 1))
                    rows = bass.ds((i * 2 + j) * P, P)
                    act.wait_ge(S1["x"][j], (i + 1) * 16)
                    layer_norm_act(act, S1, done, xw[:, j, :])
                    copy_hT(act, S1, done)
                    relu_and_store(act, S1, done, msg1[rows, :], root1[rows, :])
            act.wait_ge(S1["stored"], 2 * BLOCKS * 32 + 32)

        @block.tensor
        def _(pe):
            with pe.Fori(0, BLOCKS) as i:
                pe.wait_ge(S1["place"], i + 1)
                for k in range(BC):
                    ins = pe.matmul(pplace[:, 2 * k:2 * k + 2], place[:, k * P:(k + 1) * P], halves[:, :], start=True,
                                    stop=True)
                ins.then_inc(S1["places"], 1)
                for j in range(2):
                    done = pe.snap(i * 2 + (j + 1))
                    transpose_h(pe, S1, done)
                    project(pe, S1, done, wpr1, 2 * D)
    finish(S1)

    S2 = semaphores("sage", ["rel", "start", "moved", "merged", "sums_stored", "clip", "rcount", "mean", "mean_transposed",
                             "meanT", "lin", "o", "squares", "norm", "norm_clip", "rnorm", "h", "h_transposed", "hT", "projected",
                             "biased", "y", "stored", "x1", "stats", "mv", "var", "std", "rstd", "shift", "feats"],
                    ["idx", "dst", "rows_used", "onehot", "old", "root"])

    def sage_rounds(e):
        return e.value_load(pairs_i[0:1, 0:1], min_val=1, max_val=TILES * (GROUPS // 2) - 1)

    def each_step(e, rounds, size, body):
        with e.Fori(0, rounds) as R:
            for j in range(size):
                body(R, j, True)
        for j in range(size):
            body(rounds, j, j < size - 1)

    def group_of(e, step):
        return e.snap(step % GROUPS, min_val=0, max_val=GROUPS - 1)

    def window(e, step):
        b = e.value_load(base_i[0:1, bass.ds(group_of(e, step), 1)], min_val=0, max_val=NODES - 1)
        first = nc.s_assert_within(e.snap(b + (step // GROUPS) * P), 0, ROWS - P, skip_runtime_bounds_check_because=
                                   "a base is a node with one sweep, and zero with TILES sweeps")
        return bass.ds(first, P)

    def sage(msg, sums, rts, wl, last, gathered):
        S = S2
        per_store = 48 if last else 32
        pagg = psum[0:2]
        with nc.Block() as block:
            @block.gpsimd
            def _(pool):
                def body(R, j, ahead):
                    wait_here(pool, S["idx"][j], (R + 1) * 16)
                    wait_here(pool, S["rows_used"][j], R + 1)
                    for k in range(CHUNKS):
                        pool.indirect_dma_start(
                            out=G[:, j, k, 0:D], out_offset=None, in_=msg[0:NODES, :],
                            in_offset=bass.IndirectOffsetOnAxis(ap=idx[:, j, k:k + 1], axis=0)
                        ).then_inc(gathered[j], 16)
                each_step(pool, sage_rounds(pool), 2, body)

            @block.sync
            def _(sp):
                def load_idx(g, j):
                    sp.dma_start(idx[:, j, :], src_g[bass.ds(g, 1), :, :].rearrange("a p k -> (a p) k")
                                 ).then_inc(S["idx"][j], 16)

                def load_dst(g, j):
                    sp.dma_start(dst[:, j, :], dst_g[bass.ds(g, 1), :, :].rearrange("a p k -> (a p) k")
                                 ).then_inc(S["dst"][j], 16)

                def load_root(rows, j):
                    sp.dma_start(root[:, j, :], rts[rows, :]).then_inc(S["root"][j], 16)
                    if last:
                        sp.dma_start(xw[:, j, :], x[rows, :]).then_inc(S["root"][j], 16)

                for j in range(2):
                    load_idx(j, j)
                    load_dst(j, j)
                rows0 = window(sp, 0)
                load_root(rows0, 0)
                sp.dma_start(old[:, 0, 0:D + 1], sums[rows0, :]).then_inc(S["old"][0], 16)

                def body(R, j, ahead):
                    s = sp.snap(R * 2 + j)
                    n = 1 - j
                    g = group_of(sp, s + 2)
                    sp.wait_ge(gathered[j], (R + 1) * (16 * CHUNKS))
                    load_idx(g, j)
                    sp.wait_ge(S["onehot"][j], R + 1)
                    load_dst(g, j)
                    if not ahead:
                        return
                    rows = window(sp, s + 1)
                    sp.wait_ge(S["o"], s + 1)
                    if last:
                        sp.wait_ge(S["x1"], s + 1)
                    load_root(rows, n)
                    sp.wait_ge(S["sums_stored"], (s + 1) * 16)
                    sp.dma_start(old[:, n, 0:D + 1], sums[rows, :]).then_inc(S["old"][n], 16)
                rounds = sage_rounds(sp)
                each_step(sp, rounds, 2, body)
                for j in range(2):
                    wait_here(sp, S["idx"][j], (rounds + 2) * 16)
                    wait_here(sp, S["dst"][j], (rounds + 2) * 16)

            @block.vector
            def _(dve):
                def one_hot(j, g, nth, rounds):
                    dve.wait_ge(S["dst"][j], rounds * 16)
                    dve.tensor_scalar(dstrel[:, j, 0:CHUNKS], dst[:, j, :], base_t[:, bass.ds(g, 1)], None,
                                      ALU.subtract).then_inc(S["rel"], 1)
                    dve.wait_ge(S["rel"], nth)
                    dve.tensor_tensor(OH[:, j, 0:CHUNKS, :],
                                      dstrel[:, j, 0:CHUNKS].unsqueeze(2).to_broadcast([P, CHUNKS, P]),
                                      iota_row[:, :].unsqueeze(1).to_broadcast([P, CHUNKS, P]),
                                      ALU.is_equal).then_inc(S["onehot"][j], 1)
                    dve.tensor_scalar(base_t[:, bass.ds(g, 1)], base_t[:, bass.ds(g, 1)], float(P), None,
                                      ALU.add).then_inc(S["moved"], 1)
                    wait_here(dve, S["moved"], nth)

                dve.tensor_copy(base_t[:, :], base0_t[:, :]).then_inc(S["start"], 1)
                dve.wait_ge(S["start"], 1)
                for j in range(2):
                    one_hot(j, j, j + 1, 1)

                def body(R, j, ahead):
                    s = dve.snap(R * 2 + j)
                    done = dve.snap(s + 1)
                    dve.wait_ge(S["old"][j], (R + 1) * 16)
                    dve.wait_ge(S["rows_used"][j], R + 2)
                    dve.tensor_tensor(new[:, 0:D + 1], pagg[j][:, 0:D + 1], old[:, j, 0:D + 1],
                                      ALU.add).then_inc(S["merged"], 1)
                    dve.wait_ge(S["merged"], done)
                    dve.tensor_scalar(cnt[:, 0:1], new[:, D:D + 1], 1.0, None, ALU.max).then_inc(S["clip"], 1)
                    dve.wait_ge(S["clip"], done)
                    dve.reciprocal(cnt[:, 1:2], cnt[:, 0:1]).then_inc(S["rcount"], 1)
                    dve.wait_ge(S["rcount"], done)
                    dve.tensor_scalar(aggr[:, :], new[:, 0:D], cnt[:, 1:2], None, ALU.mult).then_inc(S["mean"], 1)
                    if ahead:
                        one_hot(j, group_of(dve, s + 2), dve.snap(s + 3), R + 2)
                    dve.wait_ge(S["lin"], done)
                    dve.wait_ge(S["root"][j], (R + 1) * (32 if last else 16))
                    dve.tensor_tensor(o[:, :], po[:, 0:D], root[:, j, :], ALU.add).then_inc(S["o"], 1)
                    dve.wait_ge(S["norm"], done)
                    dve.tensor_scalar(nrm[:, 2:3], nrm[:, 1:2], EPS_NORM, None, ALU.max).then_inc(S["norm_clip"], 1)
                    dve.wait_ge(S["norm_clip"], done)
                    dve.reciprocal(nrm[:, 3:4], nrm[:, 2:3]).then_inc(S["rnorm"], 1)
                    dve.wait_ge(S["stored"], done * per_store)
                    if last:
                        dve.wait_ge(S["rnorm"], done)
                        dve.scalar_tensor_tensor(out=x1n[:, :], in0=o[:, :], scalar=nrm[:, 3:4], in1=xw[:, j, :],
                                                 op0=ALU.mult, op1=ALU.add).then_inc(S["x1"], 1)
                        dve.wait_ge(S["x1"], done)
                        layer_norm_dve(dve, S, done, x1n[:, :])
                    else:
                        add_bias(dve, S, done, b2)
                each_step(dve, sage_rounds(dve), 2, body)

            @block.scalar
            def _(act):
                act.sem_inc(S["stored"], per_store)

                def body(R, j, ahead):
                    s = act.snap(R * 2 + j)
                    done = act.snap(s + 1)
                    rows = window(act, s)
                    act.wait_ge(S["merged"], done)
                    act.dma_start(sums[rows, :], new[:, 0:D + 1]).then_inc(S["sums_stored"], 16)
                    act.wait_ge(S["mean_transposed"], done)
                    act.copy(aT[:, :, :].rearrange("p c n -> p (c n)"), tpA[:, 0:D]).then_inc(S["meanT"], 1)
                    act.wait_ge(S["o"], done)
                    act.activation(junk[:, :], o[:, :], ACT.Square, accum_out=nrm[:, 0:1]).then_inc(S["squares"], 1)
                    act.wait_ge(S["squares"], done)
                    act.activation(nrm[:, 1:2], nrm[:, 0:1], ACT.Sqrt).then_inc(S["norm"], 1)
                    if last:
                        layer_norm_act(act, S, done, x1n[:, :])
                        copy_hT(act, S, done)
                        act.wait_ge(S["projected"], done)
                        act.wait_ge(S["stored"], done * per_store)
                        act.copy(y[:, 0:D + 2 * HEADS], py[:, 0:D + 2 * HEADS]).then_inc(S["feats"], 1)
                        act.wait_ge(S["feats"], done)
                        act.dma_start(msg3[rows, :], y[:, 0:D + HEADS]).then_inc(S["stored"], 16)
                        act.dma_start(self3[rows, :], y[:, D + HEADS:D + 2 * HEADS]).then_inc(S["stored"], 16)
                        act.dma_start(x1[rows, :], x1n[:, :]).then_inc(S["stored"], 16)
                    else:
                        act.wait_ge(S["rnorm"], done)
                        act.activation(h[:, :], o[:, :], ACT.Relu, scale=nrm[:, 3:4]).then_inc(S["h"], 1)
                        copy_hT(act, S, done)
                        relu_and_store(act, S, done, msg2[rows, :], root2[rows, :])
                rounds = sage_rounds(act)
                each_step(act, rounds, 2, body)
                steps = act.snap(rounds * 2 + 2)
                wait_here(act, S["stored"], (steps + 1) * per_store)
                wait_here(act, S["sums_stored"], steps * 16)

            @block.tensor
            def _(pe):
                for j in range(2):
                    pe.sem_inc(S["rows_used"][j], 1)

                def sum_rows(j, chunks):
                    for k in chunks:
                        ins = pe.matmul(pagg[j][:, 0:D + 1], OH[:, j, k, :], G[:, j, k, 0:D + 1], start=(k == 0),
                                        stop=(k == CHUNKS - 1))
                        if k == CHUNKS - 1:
                            ins.then_inc(S["rows_used"][j], 1)

                pe.wait_ge(S["onehot"][0], 1)
                pe.wait_ge(gathered[0], 16 * CHUNKS)
                sum_rows(0, range(CHUNKS))

                def body(R, j, ahead):
                    done = pe.snap(R * 2 + (j + 1))
                    n = 1 - j
                    if ahead:
                        pe.wait_ge(S["onehot"][n], R + (1 + j))
                        pe.wait_ge(gathered[n], (R + (1 + j)) * (16 * CHUNKS))
                        sum_rows(n, range(0, 3))
                    pe.wait_ge(S["mean"], done)
                    for c in range(2):
                        ins = pe.transpose(tpA[:, c * P:(c + 1) * P], aggr[:, c * P:(c + 1) * P], ident[:, :])
                    ins.then_inc(S["mean_transposed"], 1)
                    if ahead:
                        sum_rows(n, range(3, 5))
                    pe.wait_ge(S["meanT"], done)
                    for c in range(2):
                        ins = pe.matmul(po[:, 0:D], aT[:, c, :], wl[:, c, :], start=(c == 0), stop=(c == 1))
                    ins.then_inc(S["lin"], 1)
                    if ahead:
                        sum_rows(n, range(5, 10))
                    transpose_h(pe, S, done)
                    if ahead:
                        sum_rows(n, range(10, CHUNKS))
                    project(pe, S, done, wg if last else wpr2, D + 2 * HEADS if last else 2 * D)
                each_step(pe, sage_rounds(pe), 2, body)

    def clear(S):
        for sem in S.values():
            for one in (sem if isinstance(sem, list) else [sem]):
                nc.sync.sem_clear(one)
        nc.all_engine_barrier()

    sage(msg1, sum1, root1, wl1, False, G1["rows"])
    clear(S2)
    sage(msg2, sum2, root2, wl2, True, G2["rows"])
    finish(S2)

    recs = sb("recs", [P, RING, ACHUNKS, 4], i32)
    own = sb("own", [P, RING, HEADS])
    top = sb("top", [P, RING, HEADS])
    OT, NOT = sb("OT", [P, ACHUNKS, P], bf16), sb("NOT", [P, ACHUNKS, P], bf16)
    own3, own_r = sb("own3", [P, 3, HEADS], bf16), sb("own_r", [P, HEADS])
    z = sb("z", [P, 2, ACHUNKS, HEADS])
    E, Er = sb("E", [P, ACHUNKS, HEADS]), sb("Er", [P, ACHUNKS * HEADS])
    E3 = sb("E3", [P, ACHUNKS // PART, 3, PQ], bf16)
    ET = sb("ET", [3 * PQ, ACHUNKS // PART, P], bf16)
    cmax = sb("cmax", [P, ACHUNKS, HEADS])
    gmax, tmax = sb("gmax", [P, HEADS]), sb("tmax", [P, HEADS])
    max3, max_r = sb("max3", [P, 3, HEADS], bf16), sb("max_r", [P, HEADS])
    fade = sb("fade", [P, 2, HEADS])
    zd = sb("zd", [P, 2, ACHUNKS, HEADS])
    pr = sb("pr", [P, ACHUNKS, HEADS])
    faded = sb("faded", [P, D + HEADS])
    rden = sb("rden", [P, 2, HEADS])
    outw = sb("outw", [P, 3, D])
    NS = ACHUNKS * HEADS
    parts = "p (k i h) -> p k h i"
    by_head = "p (h o) -> p h o"
    OT_SETS = [range(a, min(a + 4, ACHUNKS)) for a in range(0, ACHUNKS, 4)]
    BY_ACT = ACHUNKS - BY_DVE
    pown, pedge, pOT, pbc, pagg = psum[0], psum[1], psum[2:4], psum[4:7], psum[7]
    pET = psum[1][:, 256:256 + ACHUNKS // PART * P // 2].bitcast(bf16)
    S3 = semaphores("gat", ["rel", "OT_out", "OT", "NOT", "own_hi", "own_r", "own_mid", "own3", "z_own", "z_sum", "z",
                            "leaky", "E", "E_hi", "E_r", "E_mid", "E3", "ET_out", "ET", "spread", "chunk_max", "gmax",
                            "tmax", "max_hi", "max_r", "max_mid", "max3", "fade_by", "fade", "m_edge", "m_sum", "below", "clipped",
                            "p", "p_den", "V_act", "V_dve", "keep", "keep_den", "merged", "den", "rden", "mean", "biased",
                            "out", "out_stored", "att_stored", "top_stored"], ["rec", "rows_used", "onehot", "own", "top", "old"],
                    RING)
    rows3 = G3["rows"]

    def rounds3(e):
        return e.value_load(rounds_i[0:1, 0:1], min_val=1, max_val=-(-MOST // RING) - 1)

    def window3(e, step):
        return bass.ds(e.value_load(base3_i[0:1, bass.ds(step, 1)], min_val=0, max_val=TILES * P), P)

    with nc.Block() as block:
        @block.gpsimd
        def _(pool):
            def body(R, j, ahead):
                wait_here(pool, S3["rec"][j], (R + 1) * 16)
                wait_here(pool, S3["rows_used"][j], R + 1)
                for k in range(ACHUNKS):
                    pool.indirect_dma_start(
                        out=G[:, j, k, 0:D + HEADS], out_offset=None, in_=msg3[0:NODES, :],
                        in_offset=bass.IndirectOffsetOnAxis(ap=recs[:, j, k, 0:1], axis=0)
                    ).then_inc(rows3[j], 16)
            each_step(pool, rounds3(pool), RING, body)

        @block.sync
        def _(sp):
            records = rec_d.rearrange("(s p k) c -> s p (k c)", p=P, k=ACHUNKS)

            def load_rec(s, j):
                sp.dma_start(recs[:, j, :, :].rearrange("p k c -> p (k c)"),
                             records[bass.ds(s, 1), :, :].rearrange("a p k -> (a p) k")).then_inc(S3["rec"][j], 16)

            for j in range(RING):
                load_rec(j, j)
            for j in range(2):
                sp.dma_start(own[:, j, :], self3[window3(sp, j), :]).then_inc(S3["own"][j], 16)
            first = window3(sp, 0)
            sp.dma_start(top[:, 0, :], att3[first, D + HEADS:D + 2 * HEADS]).then_inc(S3["top"][0], 16)
            sp.dma_start(xw[:, 0, :], x1[first, :]).then_inc(S3["old"][0], 16)
            sp.dma_start(old[:, 0, 0:D + HEADS], att3[first, 0:D + HEADS]).then_inc(S3["old"][0], 16)

            def body(R, j, ahead):
                s = sp.snap(R * RING + j)
                n, m = (j + 1) % RING, (j + 2) % RING
                rows, rows_next, rows_after = window3(sp, s), window3(sp, s + 1), window3(sp, s + 2)
                s_records = sp.snap(s + 3)
                sp.wait_ge(S3["tmax"], s + 1)
                sp.dma_start(att3[rows, D + HEADS:D + 2 * HEADS], tmax[:, :]).then_inc(S3["top_stored"], 16)
                sp.dma_start(own[:, m, :], self3[rows_after, :]).then_inc(S3["own"][m], 16)
                sp.wait_ge(rows3[j], (R + 1) * (16 * ACHUNKS))
                load_rec(s_records, j)
                sp.wait_ge(S3["top_stored"], (s + 1) * 16)
                if ahead:
                    sp.dma_start(top[:, n, :], att3[rows_next, D + HEADS:D + 2 * HEADS]).then_inc(S3["top"][n], 16)
                    sp.dma_start(xw[:, n, :], x1[rows_next, :]).then_inc(S3["old"][n], 16)
                    wait_here(sp, S3["att_stored"], (s + 1) * 16)
                    sp.dma_start(old[:, n, 0:D + HEADS], att3[rows_next, 0:D + HEADS]).then_inc(S3["old"][n], 16)
            rounds = rounds3(sp)
            each_step(sp, rounds, RING, body)
            for j in range(RING):
                wait_here(sp, S3["rec"][j], (rounds + 2) * 16)
                wait_here(sp, S3["own"][j], (rounds + (2 if j < 2 else 1)) * 16)

        def split(dve, src, three, rest, done, hi, r, mid, lo):
            dve.tensor_copy(three(0), src).then_inc(hi, 1)
            dve.wait_ge(hi, done)
            dve.tensor_tensor(rest, src, three(0), ALU.subtract).then_inc(r, 1)
            dve.wait_ge(r, done)
            dve.tensor_copy(three(1), rest).then_inc(mid, 1)
            dve.wait_ge(mid, done)
            dve.tensor_tensor(three(2), rest, three(1), ALU.subtract).then_inc(lo, 1)

        @block.vector
        def _(dve):
            Eflat = E[:, :, :].rearrange("p k h -> p (k h)")

            def one_hot(n, Rn, s, done):
                dve.wait_ge(S3["rec"][n], Rn * 16)
                dve.tensor_scalar(dstrel[:, n, :], recs[:, n, :, 1], base3_t[:, bass.ds(s, 1)], None,
                                  ALU.subtract).then_inc(S3["rel"], 1)
                dve.wait_ge(S3["rel"], done)
                dve.tensor_tensor(OH[:, n, :, :], dstrel[:, n, :].unsqueeze(2).to_broadcast([P, ACHUNKS, P]),
                                  iota_row[:, :].unsqueeze(1).to_broadcast([P, ACHUNKS, P]),
                                  ALU.is_equal).then_inc(S3["onehot"][n], 1)

            def scores(n, Rn, done):
                dve.wait_ge(S3["own"][n], Rn * 16)
                split(dve, own[:, n, :], lambda q: own3[:, q, :], own_r[:, :], done, S3["own_hi"], S3["own_r"], S3["own_mid"],
                      S3["own3"])
                dve.wait_ge(S3["OT"], done * len(OT_SETS))
                dve.tensor_scalar(NOT[:, :, :], OT[:, :, :], -1.0, 1.0, ALU.mult, ALU.add).then_inc(S3["NOT"], 1)
                dve.wait_ge(S3["z_own"], done)
                dve.tensor_reduce(z[:, 0, :, :], pown[:, 0:3 * NS].rearrange(parts, i=3, h=HEADS), axis=AX.X,
                                  op=ALU.add).then_inc(S3["z_sum"], 1)
                dve.wait_ge(S3["z_sum"], done)
                dve.wait_ge(rows3[n], Rn * (16 * ACHUNKS))
                dve.tensor_tensor(z[:, 1, :, :], z[:, 0, :, :], G[:, n, :, D:D + HEADS], ALU.add).then_inc(S3["z"], 1)
                dve.wait_ge(S3["z"], done)
                dve.scalar_tensor_tensor(out=z[:, 0, :, :], in0=z[:, 1, :, :], scalar=0.2, in1=z[:, 1, :, :],
                                         op0=ALU.mult, op1=ALU.max).then_inc(S3["leaky"], 1)
                dve.wait_ge(S3["leaky"], done)
                dve.tensor_tensor(E[:, :, :], z[:, 0, :, :],
                                  recs[:, n, :, 2:3].bitcast(f32).to_broadcast([P, ACHUNKS, HEADS]),
                                  ALU.mult).then_inc(S3["E"], 1)
                dve.wait_ge(S3["E"], done)
                split(dve, Eflat.rearrange("p (a q) -> p a q", q=PQ), lambda q: E3[:, :, q, :],
                      Er[:, :].rearrange("p (a q) -> p a q", q=PQ), done, S3["E_hi"], S3["E_r"], S3["E_mid"], S3["E3"])

            def largest(s, done):
                for k in range(ACHUNKS):
                    dve.wait_ge(S3["spread"], s * ACHUNKS + (k + 1))
                    dve.tensor_reduce(cmax[:, k, :], pbc[k % 3][:, :].rearrange("p (h e) -> p h e", h=HEADS),
                                      axis=AX.X, op=ALU.max).then_inc(S3["chunk_max"], 1)
                dve.wait_ge(S3["chunk_max"], done * ACHUNKS)
                dve.tensor_reduce(gmax[:, :], cmax[:, :, :].rearrange("p k h -> p h k"), axis=AX.X,
                                  op=ALU.max).then_inc(S3["gmax"], 1)

            one_hot(0, 1, 0, 1)
            scores(0, 1, 1)
            largest(0, 1)

            def body(R, j, ahead):
                s = dve.snap(R * RING + j)
                done = dve.snap(s + 1)
                n = (j + 1) % RING
                Rn = R + 2 if n == 0 else R + 1
                dve.wait_ge(S3["gmax"], done)
                dve.wait_ge(S3["top"][j], (R + 1) * 16)
                dve.tensor_tensor(tmax[:, :], top[:, j, :], gmax[:, :], ALU.max).then_inc(S3["tmax"], 1)
                dve.wait_ge(S3["tmax"], done)
                split(dve, tmax[:, :], lambda q: max3[:, q, :], max_r[:, :], done, S3["max_hi"], S3["max_r"], S3["max_mid"],
                      S3["max3"])
                dve.tensor_tensor(fade[:, 0, :], top[:, j, :], tmax[:, :], ALU.subtract).then_inc(S3["fade_by"], 1)
                if ahead:
                    one_hot(n, Rn, s + 1, dve.snap(s + 2))
                dve.wait_ge(S3["m_edge"], done)
                dve.tensor_reduce(zd[:, 0, :, :], pedge[:, 0:3 * NS].rearrange(parts, i=3, h=HEADS), axis=AX.X,
                                  op=ALU.add).then_inc(S3["m_sum"], 1)
                dve.wait_ge(S3["m_sum"], done)
                dve.tensor_tensor(zd[:, 1, :, :], E[:, :, :], zd[:, 0, :, :], ALU.subtract).then_inc(S3["below"], 1)
                dve.wait_ge(S3["below"], done)
                dve.tensor_scalar(zd[:, 0, :, :], zd[:, 1, :, :], 0.0, None, ALU.min).then_inc(S3["clipped"], 1)
                if ahead:
                    scores(n, Rn, dve.snap(s + 2))
                dve.wait_ge(S3["p"], done)
                dve.tensor_tensor(V[:, BY_ACT:, 0:D].rearrange("p k (h o) -> p k h o", h=HEADS),
                                  G[:, j, BY_ACT:, 0:D].rearrange("p k (h o) -> p k h o", h=HEADS),
                                  pr[:, BY_ACT:, :].unsqueeze(3).to_broadcast([P, BY_DVE, HEADS, HD]),
                                  ALU.mult).then_inc(S3["V_dve"], 1)
                dve.wait_ge(S3["fade"], done)
                dve.wait_ge(S3["old"][j], (R + 1) * 32)
                dve.tensor_tensor(faded[:, 0:D].rearrange(by_head, h=HEADS), old[:, j, 0:D].rearrange(by_head, h=HEADS),
                                  fade[:, 1, :].unsqueeze(2).to_broadcast([P, HEADS, HD]), ALU.mult).then_inc(S3["keep"], 1)
                dve.tensor_tensor(faded[:, D:], old[:, j, D:D + HEADS], fade[:, 1, :], ALU.mult).then_inc(S3["keep_den"], 1)
                if ahead:
                    largest(done, dve.snap(s + 2))
                dve.wait_ge(S3["rows_used"][j], R + 2)
                dve.wait_ge(S3["keep_den"], done)
                dve.tensor_tensor(new[:, 0:D + HEADS], pagg[:, 0:D + HEADS], faded[:, :], ALU.add).then_inc(S3["merged"], 1)
                dve.wait_ge(S3["merged"], done)
                dve.tensor_scalar(rden[:, 0, :], new[:, D:D + HEADS], 1e-30, None, ALU.max).then_inc(S3["den"], 1)
                dve.wait_ge(S3["den"], done)
                dve.reciprocal(rden[:, 1, :], rden[:, 0, :]).then_inc(S3["rden"], 1)
                dve.wait_ge(S3["rden"], done)
                dve.tensor_tensor(outw[:, 0, :].rearrange(by_head, h=HEADS), new[:, 0:D].rearrange(by_head, h=HEADS),
                                  rden[:, 1, :].unsqueeze(2).to_broadcast([P, HEADS, HD]), ALU.mult).then_inc(S3["mean"], 1)
                dve.wait_ge(S3["mean"], done)
                dve.tensor_tensor(outw[:, 1, :], outw[:, 0, :], bias_t[:, :], ALU.add).then_inc(S3["biased"], 1)
                dve.wait_ge(S3["biased"], done)
                dve.wait_ge(S3["out_stored"], done * 16)
                dve.scalar_tensor_tensor(out=outw[:, 2, :], in0=outw[:, 1, :], scalar=0.0, in1=xw[:, j, :],
                                         op0=ALU.max, op1=ALU.add).then_inc(S3["out"], 1)
            each_step(dve, rounds3(dve), RING, body)

        @block.scalar
        def _(act):
            act.sem_inc(S3["out_stored"], 16)

            def copy_OT(s1):
                for a, chunks in enumerate(OT_SETS):
                    act.wait_ge(S3["OT_out"], s1 * len(OT_SETS) + (a + 1))
                    act.copy(OT[:, chunks[0]:chunks[-1] + 1, :].rearrange("p k n -> p (k n)"),
                             pOT[a % 2][:, 0:len(chunks) * P]).then_inc(S3["OT"], 1)

            def copy_ET(done1):
                act.wait_ge(S3["ET_out"], done1)
                act.copy(ET[:, :, :].rearrange("p a n -> p (a n)"), pET[0:3 * PQ, :]).then_inc(S3["ET"], 1)

            def scale(j, chunks):
                for k in chunks:
                    for q in range(HEADS):
                        ins = act.activation(V[:, k, q * HD:(q + 1) * HD], G[:, j, k, q * HD:(q + 1) * HD], ACT.Copy,
                                             scale=pr[:, k, q:q + 1])
                    ins.then_inc(S3["V_act"], 1)

            copy_OT(0)
            copy_ET(1)

            def body(R, j, ahead):
                s = act.snap(R * RING + j)
                done = act.snap(s + 1)
                act.wait_ge(S3["fade_by"], done)
                act.activation(fade[:, 1, :], fade[:, 0, :], ACT.Exp).then_inc(S3["fade"], 1)
                if ahead:
                    copy_OT(done)
                act.wait_ge(S3["clipped"], done)
                act.activation(pr[:, :, :], zd[:, 0, :, :], ACT.Exp).then_inc(S3["p"], 1)
                act.wait_ge(S3["p"], done)
                act.copy(V[:, :, D:], pr[:, :, :]).then_inc(S3["p_den"], 1)
                scale(j, range(0, 5))
                if ahead:
                    copy_ET(act.snap(s + 2))
                scale(j, range(5, BY_ACT))
                rows = window3(act, s)
                act.wait_ge(S3["merged"], done)
                act.dma_start(att3[rows, 0:D + HEADS], new[:, 0:D + HEADS]).then_inc(S3["att_stored"], 16)
                act.wait_ge(S3["out"], done)
                act.dma_start(out[rows, :], outw[:, 2, :]).then_inc(S3["out_stored"], 16)
            rounds = rounds3(act)
            each_step(act, rounds, RING, body)
            steps = act.snap(rounds * RING + RING)
            wait_here(act, S3["att_stored"], steps * 16)
            wait_here(act, S3["out_stored"], (steps + 1) * 16)

        @block.tensor
        def _(pe):
            for j in range(RING):
                pe.sem_inc(S3["rows_used"][j], 1)

            def exchange(n, Rn, s1):
                pe.wait_ge(S3["onehot"][n], Rn)
                for a, chunks in enumerate(OT_SETS):
                    if a >= 2:
                        pe.wait_ge(S3["OT"], s1 * len(OT_SETS) + (a - 1))
                    for b, k in enumerate(chunks):
                        ins = pe.transpose(pOT[a % 2][:, b * P:(b + 1) * P], OH[:, n, k, :], ident[:, :])
                    ins.then_inc(S3["OT_out"], 1)
                pe.wait_ge(S3["own3"], s1 + 1)
                pe.wait_ge(S3["OT"], (s1 + 1) * len(OT_SETS))
                for k in range(ACHUNKS):
                    ins = pe.matmul(pown[:, k * 3 * HEADS:(k + 1) * 3 * HEADS], OT[:, k, :],
                                    own3[:, :, :].rearrange("p i h -> p (i h)"), start=True, stop=True)
                ins.then_inc(S3["z_own"], 1)

            def exchange_scores(s1):
                pe.wait_ge(S3["E3"], s1 + 1)
                for a in range(ACHUNKS // PART):
                    ins = pe.transpose(pET[0:3 * PQ, a * P:(a + 1) * P],
                                       E3[:, a, :, :].rearrange("p i q -> p (i q)"), identb[:, :])
                ins.then_inc(S3["ET_out"], 1)
                pe.wait_ge(S3["ET"], s1 + 1)
                pe.wait_ge(S3["NOT"], s1 + 1)

            def spread(s1, k):
                bank = pbc[k % 3]
                if k >= 3:
                    pe.wait_ge(S3["chunk_max"], s1 * ACHUNKS + (k - 2))
                pe.matmul(bank[:, :], negid[:, :], NOT[:, k, :].unsqueeze(1).to_broadcast([P, HEADS, P]), start=True,
                          stop=False)
                for q in range(HEADS):
                    ins = pe.matmul(bank[:, q * P:(q + 1) * P], sel[:, (k % PART) * HEADS + q, :],
                                    ET[:, k // PART, :], start=False, stop=(q == HEADS - 1))
                ins.then_inc(S3["spread"], 1)

            def sum_rows(s, done, j, k):
                if k == 0:
                    pe.wait_ge(S3["p_den"], done)
                if k < BY_ACT:
                    pe.wait_ge(S3["V_act"], s * BY_ACT + (k + 1))
                elif k == BY_ACT:
                    pe.wait_ge(S3["V_dve"], done)
                ins = pe.matmul(pagg[:, 0:D + HEADS], OH[:, j, k, :], V[:, k, :], start=(k == 0),
                                stop=(k == ACHUNKS - 1))
                if k == ACHUNKS - 1:
                    ins.then_inc(S3["rows_used"][j], 1)

            exchange(0, 1, 0)
            exchange_scores(0)
            for k in range(ACHUNKS):
                spread(0, k)

            def body(R, j, ahead):
                s = pe.snap(R * RING + j)
                done = pe.snap(s + 1)
                n = (j + 1) % RING
                pe.wait_ge(S3["max3"], done)
                for k in range(ACHUNKS):
                    ins = pe.matmul(pedge[:, k * 3 * HEADS:(k + 1) * 3 * HEADS], OT[:, k, :],
                                    max3[:, :, :].rearrange("p i h -> p (i h)"), start=True, stop=True)
                ins.then_inc(S3["m_edge"], 1)
                if ahead:
                    exchange(n, R + 2 if n == 0 else R + 1, done)
                    exchange_scores(done)
                for k in range(ACHUNKS):
                    if ahead:
                        spread(done, k)
                    sum_rows(s, done, j, k)
            each_step(pe, rounds3(pe), RING, body)


def kernel(**inputs):
    import numpy as np
    import concourse.bacc as bacc
    from concourse.bass_utils import run_bass_kernel_spmd

    def filled(a, fill):
        a = np.asarray(a)
        return np.concatenate([a, np.full(ALL * P - EDGES, fill, a.dtype)])

    def by_partition(a, blocks, chunks):
        return np.ascontiguousarray(a.reshape(blocks, chunks, P).transpose(0, 2, 1))

    def by_block(a):
        a = a.reshape(2, BLOCKS, BC, P).transpose(1, 3, 0, 2).reshape(BLOCKS, P, 2 * BC)
        return np.concatenate([a, np.zeros_like(a[:2])])

    src, dst, weight = inputs["src"], inputs["dst"], inputs["edge_weight"]
    dst_filled = filled(dst, NO_NODE)
    arrays = {"x": np.concatenate([np.asarray(inputs["x"]), np.zeros((ROWS + 2 * P - NODES, D), np.float32)]),
              "src_g": by_partition(filled(src, 0), GROUPS, CHUNKS), "dst_g": by_partition(dst_filled, GROUPS, CHUNKS),
              "dst_s": dst_filled.reshape(GROUPS, GE), "src_p": filled(src, PAD_SRC).reshape(P, ALL),
              "src_b": by_block(filled(src, PAD_SRC)), "dst_b": by_block(filled(dst, 0)),
              "w_b": by_block(filled(weight, 0))}
    for name in ("W_proj1", "b_proj1", "W_l1", "b_l1", "W_r1", "W_proj2", "b_proj2", "W_l2", "b_l2", "W_r2"):
        arrays[name] = np.ascontiguousarray(inputs[f"L0_gnn_{name}"])
    arrays["W"] = np.ascontiguousarray(inputs["L1_gnn_W"])
    for name in ("a_self", "a_neigh", "bias"):
        arrays[name] = np.ascontiguousarray(inputs[f"L1_gnn_{name}"]).reshape(-1)
    nc = bacc.Bacc("TRN2", target_bir_lowering=False, num_devices=1)
    args = [nc.dram_tensor(f"in_{n}", a.shape, mybir.dt.from_np(a.dtype), kind="ExternalInput").ap()
            for n, a in arrays.items()]
    out = nc.dram_tensor("out", [ROWS, D], mybir.dt.float32, kind="ExternalOutput").ap()
    gnn_program(nc, *args, out)
    r = run_bass_kernel_spmd(nc, [{f"in_{n}": a for n, a in arrays.items()}], core_ids=[0])
    return r.results[0]["out"][:NODES]
```

```python
import concourse.bass as bass
from concourse import mybir

NODES, D, EDGES = 6250, 256, 106250
P = 128
HEADS, HD = 4, 64
TILES = -(-NODES // P)
ROWS = 52 * P

CHUNKS = 13
GE = P * CHUNKS
GROUPS = -(-EDGES // GE)
ALL = GROUPS * CHUNKS
SPARE_T = min(t for t in range(1, 53) if (ROWS - NODES) % t == 0 and (ROWS - NODES) // t <= P)
SPARE_P = (ROWS - NODES) // SPARE_T
NO_NODE = 1 << 20

BLOCKS = 26
BC = ALL // 2 // BLOCKS
HALF_EDGES = ALL // 2 * P
PAD_SRC = TILES * P
ACHUNKS = 18
AE = P * ACHUNKS
MOST = EDGES // AE + TILES
RING = 4
MOST_ROUNDS = -(-(MOST - 1) // RING)
ASTEPS = 1 + MOST_ROUNDS * RING + RING
NEG = -1.0e30
PART = 3
PQ = PART * HEADS
HI, LO = P // 16, 16
SCORES = 3 * PQ
DIGITS = HI + LO
MIXED = SCORES + PART * DIGITS
BY_DVE = 4
GW = 264
EPS_LN, EPS_NORM = 1e-5, 1e-12


def gnn_program(nc, x, src_g, dst_g, dst_s, src_p, src_b, dst_b, w_b, Wp1, bp1, Wl1, bl1, Wr1, Wp2, bp2, Wl2, bl2,
                Wr2, W, a_self, a_neigh, bias, out):
    f32, bf16, i32 = mybir.dt.float32, mybir.dt.bfloat16, mybir.dt.int32
    ALU, ACT, AX = mybir.AluOpType, mybir.ActivationFunctionType, mybir.AxisListType

    def sb(name, shape, dt=f32):
        return nc.alloc_sbuf_tensor(name, shape, dt)

    def table(name, width):
        return nc.dram_tensor(name, [ROWS, width], f32).ap()

    def semaphores(tag, single, rings=(), size=2):
        made = {n: nc.alloc_semaphore(f"{tag}_{n}") for n in single}
        made.update({n: [nc.alloc_semaphore(f"{tag}_{n}_{j}") for j in range(size)] for n in rings})
        return made

    def finish(S):
        for sem in S.values():
            for one in (sem if isinstance(sem, list) else [sem]):
                nc.sync.sem_clear(one)
                nc.release_semaphore(one)
        nc.all_engine_barrier()

    G1 = semaphores("gather1", [], ["rows"])
    G2 = semaphores("gather2", [], ["rows"])
    G3 = semaphores("gather3", [], ["rows"], RING)
    GS = semaphores("scatter", [], ["records"])
    passed = {e.engine: nc.alloc_semaphore(f"passed_{n}") for n, e in
              (("act", nc.scalar), ("dve", nc.vector), ("pool", nc.gpsimd), ("sp", nc.sync))}

    def wait_here(e, sem, value):
        e.wait_ge(sem, value)
        e.sem_inc(passed[e.engine], 1)

    msg1, msg2 = table("msg1", D), table("msg2", D)
    msg3 = table("msg3", D + HEADS)
    sum1, sum2 = table("sum1", D + 1), table("sum2", D + 1)
    root1, root2 = table("root1", D), table("root2", D)
    x1 = table("x1", D)
    self3 = table("self3", HEADS)
    att3 = table("att3", D + 2 * HEADS)
    tile_d = nc.dram_tensor("tile_d", [2, HALF_EDGES + 2 * BC * P], bf16).ap()
    rec_d = nc.dram_tensor("rec_d", [ASTEPS * AE, 4], i32).ap()

    ident = sb("ident", [P, P])
    identb = sb("identb", [P, P], bf16)
    iota_b = sb("iota_b", [P, LO], bf16)
    iota_i = sb("iota_i", [P, P], i32)
    iota_row = sb("iota_row", [P, P])
    ones = sb("ones", [P, P])
    sel = sb("sel", [MIXED, PQ, P], bf16)
    base0_t, base_t = sb("base0_t", [P, GROUPS]), sb("base_t", [P, GROUPS])
    base_i = sb("base_i", [1, GROUPS], i32)
    pairs_i = sb("pairs_i", [1, 1], i32)
    base3_t, base3_i = sb("base3_t", [P, ASTEPS]), sb("base3_i", [1, ASTEPS], i32)
    rounds_i = sb("rounds_i", [1, 1], i32)
    wl1, wl2 = sb("wl1", [P, 2, D]), sb("wl2", [P, 2, D])
    wpr1, wpr2 = sb("wpr1", [P, 2, 2 * D]), sb("wpr2", [P, 2, 2 * D])
    b1, b2 = sb("b1", [P, 2 * D]), sb("b2", [P, 2 * D])
    wg = sb("wg", [P, 2, D + 2 * HEADS])
    bias_t = sb("bias_t", [P, D])

    G = sb("G", [P, RING, ACHUNKS, GW])
    OH = sb("OH", [P, RING, ACHUNKS, P])
    idx = sb("idx", [P, 2, CHUNKS], i32)
    dst = sb("dst", [P, 2, CHUNKS], i32)
    dstrel = sb("dstrel", [P, RING, ACHUNKS])
    old = sb("old", [P, RING, D + 2 * HEADS])
    root = sb("root", [P, 2, D])
    xw = sb("xw", [P, RING, D])
    new = sb("new", [P, D + 2 * HEADS])
    cnt = sb("cnt", [P, 2])
    aggr = sb("aggr", [P, D])
    aT = sb("aT", [P, 2, P])
    o = sb("o", [P, D])
    junk = sb("junk", [P, D])
    nrm = sb("nrm", [P, 4])
    stats, mv, rs = sb("stats", [P, 6]), sb("mv", [P, 2]), sb("rs", [P, 4])
    h = sb("h", [P, D])
    hT = sb("hT", [P, 2, P])
    y = sb("y", [P, 2 * D])
    x1n = sb("x1n", [P, D])
    Gflat = G[:, :, :, :].rearrange("p a k w -> p (a k w)")
    psum = [nc.alloc_psum_tensor(f"bank{i}", [P, 512], f32) for i in range(8)]
    tpA, tpH, po, py = psum[2], psum[3], psum[4], psum[5]

    S0 = semaphores("prep", ["w", "ident", "iota", "const", "dsts", "srcs", "ready", "mm", "chain", "diag", "zero", "zeroed",
                             "tri", "tiles", "counted", "counts", "groups", "digits", "outer",
                             "starts", "cmp", "bases"])
    n_of = {}
    dsts = OH[:, 0, :, :].rearrange("p k n -> p (k n)").bitcast(i32)[0:GROUPS, 0:GE]
    srcs, tile_i = Gflat[:, 0:ALL].bitcast(i32), Gflat[:, ALL:2 * ALL].bitcast(i32)
    tile_b = sb("tile_b", [P, ALL], bf16)
    CG = P // 8
    digit_i = Gflat[:, 2 * ALL:4 * ALL].bitcast(i32).rearrange("p (d n) -> p d n", d=2)
    digit_b = Gflat[:, 4 * ALL:5 * ALL].bitcast(bf16).rearrange("p (d n) -> p d n", d=2)
    digit_is = Gflat[:, 5 * ALL:13 * ALL].bitcast(bf16).rearrange("p (d g v c) -> p d g v c", d=2, v=8, c=CG)
    column_i, column_f = sb("column_i", [P, P], i32), sb("column_f", [P, P])
    part2_i, part2_f = sb("part2_i", [P, 2], i32), sb("part2_f", [P, 2])
    high_is = sb("high_is", [P, 8])
    same = sb("same", [P, P])
    by_low = sb("by_low", [P, 2, 8])
    by_tile = sb("by_tile", [P, 2, 2, 8, 8])
    outer = psum[4:6]
    mm_f = sb("mm_f", [GROUPS, 2])
    dg = sb("dg", [GROUPS, 2, GROUPS])
    bt = sb("bt", [P, 4, GROUPS])
    flag = sb("flag", [P, 2])
    abc = sb("abc", [P, 2, D])
    tri = sb("tri", [P, P])
    before49 = sb("before49", [P, P])
    halves = sb("halves", [P, 2])
    cnt2 = sb("cnt2", [P, 4])
    ngroups = sb("ngroups", [P, 4])
    cmp = sb("cmp", [P, ASTEPS])
    rnd = sb("rnd", [P, 4])
    scan0 = sb("scan0", [P, 1])
    part_i, part_f, tile_p = sb("part_i", [P, 1], i32), sb("part_f", [P, 1]), sb("tile_p", [P, 1])
    sizes_t = sb("sizes_t", [P, ASTEPS])
    first_row = sb("first_row", [P, D + 2 * HEADS])
    zeros_b = sb("zeros_b", [2, BC * 2 * P], bf16)
    empty = OH[:, 1:3, :, :].rearrange("p a k n -> p (a k n)").bitcast(i32)
    with nc.Block() as block:
        @block.sync
        def _(sp):
            sp.dma_start(srcs[:, :], src_p).then_inc(S0["srcs"], 16)
            sp.dma_start(dsts, dst_s).then_inc(S0["dsts"], 16)
            sp.wait_ge(S0["tiles"], 1)
            for half in range(2):
                sp.dma_start(tile_d[half, 0:HALF_EDGES].rearrange("(p n) -> p n", p=P // 2),
                             tile_b[half * (P // 2):(half + 1) * (P // 2), :]).then_inc(S0["zeroed"], 16)
            n = 0
            for c in range(2):
                rows = slice(c * P, (c + 1) * P)
                for to, of in ((wl1[:, c, :], Wl1[rows, :]), (wl2[:, c, :], Wl2[rows, :]),
                               (wpr1[:, c, 0:D], Wp1[rows, :]), (wpr1[:, c, D:2 * D], Wr1[rows, :]),
                               (wpr2[:, c, 0:D], Wp2[rows, :]), (wpr2[:, c, D:2 * D], Wr2[rows, :]),
                               (wg[:, c, 0:D].rearrange("p (h o) -> p h o", h=HEADS),
                                W[:, rows, :].rearrange("h p o -> p h o"))):
                    sp.dma_start(to, of).then_inc(S0["w"], 16)
                    n += 1
            for to, of in ((b1[:, 0:D], bp1), (b1[:, D:2 * D], bl1), (b2[:, 0:D], bp2), (b2[:, D:2 * D], bl2),
                           (abc[:, 0, :], a_neigh), (abc[:, 1, :], a_self), (bias_t[:, :], bias)):
                sp.dma_start(to, of.rearrange("(a n) -> a n", a=1).to_broadcast([P, D])).then_inc(S0["w"], 16)
                n += 1
            n_of["weights"] = n
            sp.wait_ge(S0["zero"], 5)
            sp.dma_start(tile_d[:, HALF_EDGES:], zeros_b[:, :]).then_inc(S0["zeroed"], 16)
            rec_w = rec_d.rearrange("(p n) c -> p (n c)", p=P)
            at, width, pieces = 0, ASTEPS * AE * 4 // P, 0
            while at < width:
                m = min(empty.shape[1], width - at)
                sp.dma_start(rec_w[:, at:at + m], empty[:, 0:m]).then_inc(S0["zeroed"], 16)
                at, pieces = at + m, pieces + 1
            n_of["zeroed"] = 3 + pieces
            sp.wait_ge(S0["zeroed"], 16 * n_of["zeroed"])
            sp.wait_ge(S0["dsts"], 16)
            sp.wait_ge(S0["w"], 16 * n)

        @block.gpsimd
        def _(pool):
            pool.memset(ident[:, :], 0.0).then_inc(S0["ident"], 1)
            pool.wait_ge(S0["ident"], 1)
            pool.affine_select(out=ident[:, :], in_=ident[:, :], compare_op=ALU.not_equal, fill=1.0, base=0,
                               pattern=[[-1, P]], channel_multiplier=1).then_inc(S0["ident"], 1)
            slots = empty.rearrange("p (n c) -> p n c", c=4)
            pool.memset(empty, 0).then_inc(S0["zero"], 1)
            pool.memset(zeros_b[:, :], 0.0).then_inc(S0["zero"], 1)
            pool.wait_ge(S0["zero"], 1)
            pool.memset(slots[:, :, 1:2].bitcast(f32), float(NO_NODE)).then_inc(S0["zero"], 1)
            pool.memset(slots[:, :, 3:4].bitcast(bf16), float(P)).then_inc(S0["zero"], 1)
            pool.memset(first_row[:, 0:D + HEADS], 0.0)
            pool.memset(first_row[:, D + HEADS:], NEG).then_inc(S0["zero"], 1)
            pool.iota(iota_i[:, :], [[1, P]], base=0, channel_multiplier=0).then_inc(S0["iota"], 1)
            pool.iota(part_i[:, :], [[0, 1]], base=0, channel_multiplier=1).then_inc(S0["iota"], 1)
            pool.memset(tri[:, :], 1.0).then_inc(S0["tri"], 1)
            pool.memset(before49[:, :], 1.0).then_inc(S0["tri"], 1)
            pool.memset(halves[:, :], 1.0).then_inc(S0["tri"], 1)
            pool.wait_ge(S0["tri"], 3)
            pool.affine_select(out=tri[:, :].rearrange("p (a m) -> p a m", a=2),
                               in_=tri[:, :].rearrange("p (a m) -> p a m", a=2), compare_op=ALU.is_ge, fill=0.0,
                               base=-1, pattern=[[0, 2], [1, P // 2]], channel_multiplier=-1).then_inc(S0["tri"], 1)
            pool.affine_select(out=before49[:, :], in_=before49[:, :], compare_op=ALU.is_ge, fill=0.0,
                               base=TILES - 1, pattern=[[0, P]], channel_multiplier=-1).then_inc(S0["tri"], 1)
            pool.affine_select(out=halves[:, 0:1], in_=halves[:, 0:1], compare_op=ALU.is_ge, fill=0.0,
                               base=P // 2 - 1, pattern=[[0, 1]], channel_multiplier=-1).then_inc(S0["tri"], 1)
            pool.affine_select(out=halves[:, 1:2], in_=halves[:, 1:2], compare_op=ALU.is_ge, fill=0.0,
                               base=-P // 2, pattern=[[0, 1]], channel_multiplier=1).then_inc(S0["tri"], 1)
            pool.memset(sel[:, :, :], 0.0).then_inc(S0["const"], 1)
            for part in range(3):
                pool.wait_ge(S0["const"], part + 1)
                pool.affine_select(out=sel[:, :, :], in_=sel[:, :, :], compare_op=ALU.not_equal, fill=1.0,
                                   base=-part * PQ, pattern=[[-1, PQ], [0, P]],
                                   channel_multiplier=1).then_inc(S0["const"], 1)
            for c in range(PART):
                of = sel[:, c * HEADS:(c + 1) * HEADS, :].rearrange("p h (a b) -> p h a b", a=HI)
                row = SCORES + c * DIGITS
                pool.wait_ge(S0["const"], 4 + 2 * c)
                pool.affine_select(out=of, in_=of, compare_op=ALU.not_equal, fill=NEG, base=-row,
                                   pattern=[[0, HEADS], [-1, HI], [0, LO]],
                                   channel_multiplier=1).then_inc(S0["const"], 1)
                pool.wait_ge(S0["const"], 5 + 2 * c)
                pool.affine_select(out=of, in_=of, compare_op=ALU.not_equal, fill=NEG, base=-row - HI,
                                   pattern=[[0, HEADS], [0, HI], [-1, LO]],
                                   channel_multiplier=1).then_inc(S0["const"], 1)

        @block.vector
        def _(dve):
            chained = [0]

            def link(ins):
                chained[0] += 1
                ins.then_inc(S0["chain"], 1)
                dve.wait_ge(S0["chain"], chained[0])

            dve.wait_ge(S0["srcs"], 16)
            link(dve.tensor_scalar(tile_i[:, :], srcs[:, :], 7, None, ALU.logical_shift_right))
            link(dve.tensor_copy(tile_b[:, :], tile_i[:, :]))
            dve.sem_inc(S0["tiles"], 1)
            dve.memset(ones[:, :], 1.0).then_inc(S0["ready"], 1)
            link(dve.tensor_scalar(digit_i[:, 0, :], srcs, 10, None, ALU.logical_shift_right))
            link(dve.tensor_scalar(digit_i[:, 1, :], srcs, 7, 7, ALU.logical_shift_right, ALU.bitwise_and))
            for d in range(2):
                link(dve.tensor_copy(digit_b[:, d, :], digit_i[:, d, :]))
            for v in range(8):
                for d in range(2):
                    ins = dve.tensor_scalar(digit_is[:, d, :, v, :], digit_b[:, d, :].rearrange("p (g c) -> p g c", c=CG),
                                            float(v), None, ALU.is_equal)
            ins.then_inc(S0["digits"], 1)
            dve.wait_ge(S0["iota"], 2)
            link(dve.tensor_scalar(column_i[:, :], iota_i[:, :], CG - 1, None, ALU.bitwise_and))
            link(dve.tensor_scalar(part2_i[:, 0:1], part_i[:, :], CG - 1, None, ALU.bitwise_and))
            link(dve.tensor_scalar(part2_i[:, 1:2], part_i[:, :], 4, None, ALU.logical_shift_right))
            link(dve.tensor_copy(column_f[:, :], column_i[:, :]))
            link(dve.tensor_copy(part2_f[:, :], part2_i[:, :]))
            link(dve.tensor_copy(iota_row[:, :], iota_i[:, :]))
            link(dve.tensor_scalar(column_f[:, :], column_f[:, :], part2_f[:, 0:1], None, ALU.is_equal))
            link(dve.tensor_scalar(high_is[:, :], iota_row[:, 0:8], part2_f[:, 1:2], None, ALU.is_equal))
            dve.wait_ge(S0["outer"], 1)
            for half in range(2):
                link(dve.tensor_tensor(same[:, :], outer[half][:, 0:P], column_f[:, :], ALU.mult))
                link(dve.tensor_reduce(by_low[:, half, :], same[:, :].rearrange("p (b c) -> p b c", c=CG), axis=AX.X,
                                       op=ALU.add))
                for twice in range(2):
                    link(dve.tensor_tensor(by_tile[:, half, twice, :, :], high_is[:, :].unsqueeze(2).to_broadcast([P, 8, 8]),
                                           by_low[:, half, :].unsqueeze(1).to_broadcast([P, 8, 8]), ALU.mult))
            dve.sem_inc(S0["counted"], 1)
            dve.wait_ge(S0["ident"], 2)
            link(dve.tensor_copy(identb[:, :], ident[:, :]))
            link(dve.tensor_copy(iota_b[:, :], iota_i[:, 0:LO]))
            dve.wait_ge(S0["counts"], 1)
            link(dve.tensor_copy(cnt2[:, 0:2], psum[1][:, 0:2]))
            link(dve.tensor_tensor(cnt2[:, 2:3], cnt2[:, 0:1], cnt2[:, 1:2], ALU.add))
            link(dve.tensor_scalar(sizes_t[:, :], iota_row[:, 0:ASTEPS], float(AE), None, ALU.mult))
            link(dve.tensor_scalar(cmp[:, :], sizes_t[:, :], cnt2[:, 2:3], None, ALU.is_lt, ALU.add,
                                   accum_out=ngroups[:, 0:1]))
            link(dve.tensor_scalar(ngroups[:, 1:2], ngroups[:, 0:1], 1.0, None, ALU.max))
            dve.sem_inc(S0["groups"], 1)
            dve.wait_ge(S0["starts"], 1)
            link(dve.tensor_copy(rnd[:, 0:2], psum[2][:, 0:2]))
            dve.wait_ge(S0["tri"], 7)
            link(dve.tensor_copy(part_f[:, :], part_i[:, :]))
            link(dve.scalar_tensor_tensor(out=tile_p[:, :], in0=halves[:, 1:2], scalar=-float(P // 2), in1=part_f[:, :],
                                          op0=ALU.mult, op1=ALU.add))
            link(dve.tensor_tensor(rnd[:, 2:3], cnt2[:, 0:1], halves[:, 1:2], ALU.mult))
            link(dve.scalar_tensor_tensor(out=scan0[:, :], in0=rnd[:, 0:1], scalar=float(AE), in1=rnd[:, 2:3],
                                          op0=ALU.mult, op1=ALU.add))
            link(dve.tensor_scalar(cmp[:, :], iota_row[:, 0:ASTEPS], rnd[:, 0:1], None, ALU.is_ge))
            dve.sem_inc(S0["cmp"], 1)
            dve.wait_ge(S0["bases"], 1)
            link(dve.tensor_scalar(base3_t[:, :], psum[3][:, 0:ASTEPS], -1.0, float(P), ALU.add, ALU.mult))
            link(dve.tensor_copy(base3_i[:, :], base3_t[0:1, :]))
            link(dve.tensor_scalar(sizes_t[:, :], iota_row[:, 0:ASTEPS], float(RING), 1.0, ALU.mult, ALU.add))
            link(dve.tensor_scalar(cmp[:, :], sizes_t[:, :], rnd[:, 1:2], None, ALU.is_lt, ALU.add,
                                   accum_out=rnd[:, 3:4]))
            link(dve.tensor_scalar(rounds_i[:, :], rnd[0:1, 3:4], -1.0, None, ALU.add))

        @block.tensor
        def _(pe):
            pe.wait_ge(S0["ready"], 1)
            pe.wait_ge(S0["tri"], 7)
            pe.wait_ge(S0["digits"], 1)
            for half in range(2):
                of = slice(half * (P // 2), (half + 1) * (P // 2))
                for g in range(ALL // CG):
                    ins = pe.matmul(outer[half][:, 0:P], digit_is[of, 0, g, :, :].rearrange("p v c -> p (v c)"),
                                    digit_is[of, 1, g, :, :].rearrange("p v c -> p (v c)"), start=(g == 0),
                                    stop=(g == ALL // CG - 1))
            ins.then_inc(S0["outer"], 1)
            pe.wait_ge(S0["counted"], 1)
            for half in range(2):
                ins = pe.matmul(psum[1][:, half:half + 1], by_tile[:, half, :, :, :].rearrange("p t a b -> p (t a b)"),
                                ones[:, 0:1], start=True, stop=True)
            ins.then_inc(S0["counts"], 1)
            pe.wait_ge(S0["groups"], 1)
            pe.matmul(psum[2][:, 0:1], tri[:, :], ngroups[:, 1:2], start=True, stop=True)
            pe.matmul(psum[2][:, 1:2], before49[:, :], ngroups[:, 1:2], start=True, stop=True).then_inc(S0["starts"], 1)
            pe.wait_ge(S0["cmp"], 1)
            pe.matmul(psum[3][:, 0:ASTEPS], ones[0:TILES + 1, :], cmp[0:TILES + 1, :], start=True,
                      stop=True).then_inc(S0["bases"], 1)
    finish(S0)

    def transpose_h(pe, S, done):
        pe.wait_ge(S["h"], done)
        for c in range(2):
            ins = pe.transpose(tpH[:, c * P:(c + 1) * P], h[:, c * P:(c + 1) * P], ident[:, :])
        ins.then_inc(S["h_transposed"], 1)

    def copy_hT(act, S, done):
        act.wait_ge(S["h_transposed"], done)
        act.copy(hT[:, :, :].rearrange("p c n -> p (c n)"), tpH[:, 0:D]).then_inc(S["hT"], 1)

    def project(pe, S, done, weights, width):
        pe.wait_ge(S["hT"], done)
        for c in range(2):
            ins = pe.matmul(py[:, 0:width], hT[:, c, :], weights[:, c, :], start=(c == 0), stop=(c == 1))
        ins.then_inc(S["projected"], 1)

    def layer_norm_dve(dve, S, done, rows):
        dve.bn_stats(stats[:, :], rows).then_inc(S["stats"], 1)
        wait_here(dve, S["stats"], done)
        dve.bn_aggr(mv[:, :], stats[:, :]).then_inc(S["mv"], 1)
        dve.wait_ge(S["mv"], done)
        dve.tensor_scalar(rs[:, 0:1], mv[:, 1:2], EPS_LN, None, ALU.add).then_inc(S["var"], 1)
        dve.wait_ge(S["std"], done)
        dve.reciprocal(rs[:, 2:3], rs[:, 1:2]).then_inc(S["rstd"], 1)
        dve.wait_ge(S["rstd"], done)
        dve.scalar_tensor_tensor(out=rs[:, 3:4], in0=mv[:, 0:1], scalar=-1.0, in1=rs[:, 2:3], op0=ALU.mult,
                                 op1=ALU.mult).then_inc(S["shift"], 1)

    def layer_norm_act(act, S, done, rows):
        act.wait_ge(S["var"], done)
        act.activation(rs[:, 1:2], rs[:, 0:1], ACT.Sqrt).then_inc(S["std"], 1)
        act.wait_ge(S["shift"], done)
        act.activation(h[:, :], rows, ACT.Relu, bias=rs[:, 3:4], scale=rs[:, 2:3]).then_inc(S["h"], 1)

    def add_bias(dve, S, done, b):
        dve.wait_ge(S["projected"], done)
        dve.tensor_tensor(y[:, :], py[:, :], b[:, :], ALU.add).then_inc(S["biased"], 1)

    def relu_and_store(act, S, done, msg, rt):
        act.wait_ge(S["biased"], done)
        act.activation(y[:, 0:D], y[:, 0:D], ACT.Relu).then_inc(S["y"], 1)
        act.wait_ge(S["y"], done)
        act.dma_start(msg, y[:, 0:D]).then_inc(S["stored"], 16)
        act.dma_start(rt, y[:, D:2 * D]).then_inc(S["stored"], 16)

    S1 = semaphores("first", ["stats", "mv", "var", "std", "rstd", "shift", "h", "h_transposed", "hT", "projected",
                              "biased", "y", "stored", "member", "running", "place", "places", "carried",
                              "start", "digits",
                              "chain", "diag", "mm", "zeroed"], ["x", "tiles", "edges", "records", "place_i", "free"])
    BN = BC * P
    trow = Gflat[:, 0:BN].bitcast(bf16).rearrange("p (q n) -> p q n", q=2)
    member = Gflat[:, BN:BN + BN // 2].bitcast(bf16)
    zero_b = Gflat[:, BN + BN // 2:2 * BN].bitcast(bf16)
    running, place = Gflat[:, 2 * BN:3 * BN], Gflat[:, 3 * BN:4 * BN]
    digits_i = sb("digits_i", [P, 3, 2 * BC], i32)
    place_i = sb("place_i", [P, 2, BC, 2], i32)
    edges_i = sb("edges_i", [P, 2, 3, 2 * BC], i32)
    rec = sb("rec", [P, 2, 2 * BC, 4], i32)
    pplace = psum[6]
    with nc.Block() as block:
        @block.sync
        def _(sp):
            def load_x(tile, j):
                sp.dma_start(xw[:, j, :], x[bass.ds(tile * P, P), :]).then_inc(S1["x"][j], 16)

            def load_edges(i, q):
                for half in range(2):
                    sp.dma_start(trow[half * (P // 2):(half + 1) * (P // 2), q, :],
                                 tile_d[half:half + 1, bass.ds(i * BN, BN)].to_broadcast([P // 2, BN])
                                 ).then_inc(S1["tiles"][q], 16)
                for n, of in enumerate((dst_b, src_b, w_b)):
                    to = edges_i[:, q, n, :]
                    sp.dma_start(to if n < 2 else to.bitcast(f32),
                                 of[bass.ds(i, 1), :, :].rearrange("a p k -> (a p) k")).then_inc(S1["edges"][q], 16)

            for j in range(2):
                sp.sem_inc(S1["free"][j], 1)
                load_x(j, j)
                load_edges(j, j)
            for t, width in ((x1, D), (self3, HEADS)):
                sp.dma_start(t[NODES:, :].rearrange("(t p) d -> p t d", t=SPARE_T),
                             first_row[0:SPARE_P, 0:width].unsqueeze(1).to_broadcast([SPARE_P, SPARE_T, width])
                             ).then_inc(S1["zeroed"], 16)
            with sp.Fori(0, BLOCKS // 2) as i:
                for q in range(2):
                    tile = sp.snap(i * 4 + 2 * q)
                    block_next, rounds_done = sp.snap(i * 2 + (q + 2)), sp.snap(i + 1)
                    scattered = sp.snap(rounds_done * (2 * BC * 16))
                    for j in range(2):
                        tile_next = sp.snap(tile + (j + 2))
                        sp.wait_ge(S1["h"], tile + (j + 1))
                        load_x(tile_next, j)
                    wait_here(sp, S1["member"], i * 2 + (q + 1))
                    sp.wait_ge(S1["records"][q], rounds_done)
                    load_edges(block_next, q)
                    for of, width in ((att3, D + 2 * HEADS), (sum1, D + 1), (sum2, D + 1)):
                        sp.dma_start(of[bass.ds(tile * P, 2 * P), :].rearrange("(t p) d -> p t d", t=2),
                                     first_row[:, 0:width].unsqueeze(1).to_broadcast([P, 2, width])
                                     ).then_inc(S1["zeroed"], 16)
                    sp.wait_ge(GS["records"][q], scattered)
                    sp.sem_inc(S1["free"][q], 1)
            sp.wait_ge(S1["zeroed"], (2 + 3 * BLOCKS) * 16)
            for j in range(2):
                sp.wait_ge(S1["x"][j], (BLOCKS + 1) * 16)
                sp.wait_ge(S1["tiles"][j], (BLOCKS // 2 + 1) * 32)
                sp.wait_ge(S1["edges"][j], (BLOCKS // 2 + 1) * 48)

        @block.gpsimd
        def _(pool):
            with pool.Fori(0, BLOCKS // 2) as i:
                for q in range(2):
                    wait_here(pool, S1["place_i"][q], i + 1)
                    wait_here(pool, S1["records"][q], i + 1)
                    for k in range(2 * BC):
                        pool.indirect_dma_start(
                            out=rec_d[:, :], out_offset=bass.IndirectOffsetOnAxis(
                                ap=place_i[:, q, k % BC, k // BC:k // BC + 1], axis=0),
                            in_=rec[:, q, k, :], in_offset=None).then_inc(GS["records"][q], 16)
            for q in range(2):
                wait_here(pool, GS["records"][q], BLOCKS // 2 * 2 * BC * 16)

        @block.vector
        def _(dve):
            dve.memset(zero_b[:, :], 0.0).then_inc(S1["start"], 1)
            dve.memset(rec[:, :, :, :], 0).then_inc(S1["start"], 1)
            dve.wait_ge(S1["start"], 2)

            def sort_block(i, q, d):
                dve.wait_ge(S1["tiles"][q], (i + 1) * 32)
                dve.tensor_scalar(member[:, :], trow[:, q, :], tile_p[:, 0:1], None, ALU.is_equal).then_inc(S1["member"], 1)
                dve.wait_ge(S1["member"], d)
                dve.tensor_tensor_scan(out=running[:, :], data0=member[:, :], data1=zero_b[:, :],
                                       initial=scan0[:, 0:1], op0=ALU.add, op1=ALU.add).then_inc(S1["running"], 1)
                dve.wait_ge(S1["running"], d)
                dve.scalar_tensor_tensor(out=place[:, :], in0=running[:, :], scalar=-1.0, in1=member[:, :],
                                         op0=ALU.add, op1=ALU.mult).then_inc(S1["place"], 1)
                dve.tensor_copy(scan0[:, :], running[:, BN - 1:BN]).then_inc(S1["carried"], 1)
                dve.wait_ge(S1["carried"], d)

            with dve.Fori(0, BLOCKS // 2) as i:
                for q in range(2):
                    d = dve.snap(i * 2 + (q + 1))
                    sort_block(i, q, d)
                    for j in range(2):
                        tile = dve.snap(i * 4 + (2 * q + j))
                        done = dve.snap(tile + 1)
                        dve.wait_ge(S1["x"][j], d * 16)
                        layer_norm_dve(dve, S1, done, xw[:, j, :])
                        if j == 0:
                            dve.wait_ge(S1["edges"][q], (i + 1) * 48)
                            dve.wait_ge(S1["free"][q], i + 1)
                            dve.wait_ge(S1["places"], d)
                            dve.tensor_copy(place_i[:, q, :, :].rearrange("p k a -> p (k a)"),
                                            pplace[:, 0:2 * BC]).then_inc(S1["place_i"][q], 1)
                            dve.tensor_scalar(digits_i[:, 0, :], edges_i[:, q, 1, :], P - 1, None, ALU.bitwise_and)
                            dve.tensor_scalar(digits_i[:, 1, :], edges_i[:, q, 1, :], LO - 1, None, ALU.bitwise_and)
                            dve.tensor_scalar(digits_i[:, 2, :], edges_i[:, q, 1, :], 4, HI - 1,
                                              ALU.logical_shift_right, ALU.bitwise_and).then_inc(S1["digits"], 1)
                            for n in (0, 2):
                                dve.tensor_copy(rec[:, q, :, n], edges_i[:, q, n, :])
                            dve.wait_ge(S1["digits"], d)
                            dve.tensor_copy(rec[:, q, :, 1:2].bitcast(f32), digits_i[:, 0, :].unsqueeze(2))
                            for n in range(2):
                                ins = dve.tensor_copy(rec[:, q, :, 3:4].bitcast(bf16)[:, :, n:n + 1],
                                                      digits_i[:, n + 1, :].unsqueeze(2))
                            ins.then_inc(S1["records"][q], 1)
                        dve.wait_ge(S1["stored"], tile * 32 + 32)
                        add_bias(dve, S1, done, b1)

            chained = [0]

            def link(ins):
                chained[0] += 1
                ins.then_inc(S1["chain"], 1)
                dve.wait_ge(S1["chain"], chained[0])

            link(dve.tensor_reduce(mm_f[:, 0:1], dsts, axis=AX.X, op=ALU.min))
            link(dve.tensor_reduce(mm_f[:, 1:2], dsts, axis=AX.X, op=ALU.max))
            link(dve.tensor_scalar(mm_f[:, 1:2], mm_f[:, 1:2], float(NODES - 1), None, ALU.min))
            for k in range(2):
                dve.tensor_scalar(dg[:, k, :], ident[0:GROUPS, 0:GROUPS], mm_f[:, k:k + 1], None,
                                  ALU.mult).then_inc(S1["diag"], 1)
            dve.wait_ge(S1["mm"], 1)
            lo, hi = bt[:, 0, :], bt[:, 1, :]
            link(dve.tensor_copy(lo, psum[0][:, 0:GROUPS]))
            link(dve.tensor_copy(hi, psum[0][:, GROUPS:2 * GROUPS]))
            link(dve.tensor_tensor(bt[:, 2, :], hi, lo, ALU.subtract))
            link(dve.tensor_scalar(bt[:, 2, :], bt[:, 2, :], float(P - 1), None, ALU.is_le))
            link(dve.tensor_tensor(bt[:, 3, 0:GROUPS - 1], bt[:, 0, 1:GROUPS], bt[:, 0, 0:GROUPS - 1], ALU.subtract))
            link(dve.tensor_scalar(bt[:, 3, 0:GROUPS - 1], bt[:, 3, 0:GROUPS - 1], float(P), None, ALU.is_le))
            link(dve.tensor_scalar(bt[:, 3, GROUPS - 1:GROUPS], bt[:, 0, GROUPS - 1:GROUPS], float(NODES - P), None,
                                   ALU.is_ge))
            link(dve.tensor_tensor(bt[:, 2, :], bt[:, 2, :], bt[:, 3, :], ALU.mult))
            link(dve.tensor_scalar(bt[:, 3, 0:1], bt[:, 0, 0:1], 0.0, None, ALU.is_le))
            link(dve.tensor_tensor(bt[:, 2, 0:1], bt[:, 2, 0:1], bt[:, 3, 0:1], ALU.mult))
            link(dve.tensor_reduce(flag[:, 0:1], bt[:, 2, :], axis=AX.X, op=ALU.min))
            link(dve.tensor_scalar(flag[:, 1:2], flag[:, 0:1], float((1 - TILES) * (GROUPS // 2)),
                                   float(TILES * (GROUPS // 2) - 1), ALU.mult, ALU.add))
            link(dve.tensor_copy(pairs_i[:, :], flag[0:1, 1:2]))
            link(dve.tensor_scalar(base0_t[:, :], lo, flag[:, 0:1], None, ALU.mult))
            link(dve.tensor_copy(base_i[:, :], base0_t[0:1, :]))
            for k in range(2):
                for c in range(2):
                    link(dve.tensor_tensor(junk[:, :], wg[:, c, 0:D], abc[:, k, :], ALU.mult))
                    link(dve.tensor_reduce(wg[:, c, D + k * HEADS:D + (k + 1) * HEADS],
                                           junk[:, :].rearrange("p (h o) -> p h o", h=HEADS), axis=AX.X, op=ALU.add))

        @block.scalar
        def _(act):
            act.sem_inc(S1["stored"], 32)
            with act.Fori(0, BLOCKS) as i:
                for j in range(2):
                    done = act.snap(i * 2 + (j + 1))
                    rows = bass.ds((i * 2 + j) * P, P)
                    act.wait_ge(S1["x"][j], (i + 1) * 16)
                    layer_norm_act(act, S1, done, xw[:, j, :])
                    copy_hT(act, S1, done)
                    relu_and_store(act, S1, done, msg1[rows, :], root1[rows, :])
            act.wait_ge(S1["stored"], 2 * BLOCKS * 32 + 32)

        @block.tensor
        def _(pe):
            with pe.Fori(0, BLOCKS) as i:
                pe.wait_ge(S1["place"], i + 1)
                for k in range(BC):
                    ins = pe.matmul(pplace[:, 2 * k:2 * k + 2], place[:, k * P:(k + 1) * P], halves[:, :], start=True,
                                    stop=True)
                ins.then_inc(S1["places"], 1)
                for j in range(2):
                    done = pe.snap(i * 2 + (j + 1))
                    transpose_h(pe, S1, done)
                    project(pe, S1, done, wpr1, 2 * D)
            pe.wait_ge(S1["diag"], 2)
            pe.matmul(psum[0][:, 0:2 * GROUPS], ones[0:GROUPS, :], dg[:, :, :].rearrange("p a b -> p (a b)"),
                      start=True, stop=True).then_inc(S1["mm"], 1)
    finish(S1)

    S2 = semaphores("sage", ["rel", "start", "moved", "merged", "sums_stored", "clip", "rcount", "mean", "mean_transposed",
                             "meanT", "lin", "o", "squares", "norm", "norm_clip", "rnorm", "h", "h_transposed", "hT", "projected",
                             "biased", "y", "stored", "x1", "stats", "mv", "var", "std", "rstd", "shift", "feats"],
                    ["idx", "dst", "rows_used", "onehot", "old", "root"])

    def sage_rounds(e):
        return e.value_load(pairs_i[0:1, 0:1], min_val=1, max_val=TILES * (GROUPS // 2) - 1)

    def each_step(e, rounds, size, body):
        with e.Fori(0, rounds) as R:
            for j in range(size):
                body(R, j, True)
        for j in range(size):
            body(rounds, j, j < size - 1)

    def group_of(e, step):
        return e.snap(step % GROUPS, min_val=0, max_val=GROUPS - 1)

    def window(e, step):
        b = e.value_load(base_i[0:1, bass.ds(group_of(e, step), 1)], min_val=0, max_val=NODES - 1)
        first = nc.s_assert_within(e.snap(b + (step // GROUPS) * P), 0, ROWS - P, skip_runtime_bounds_check_because=
                                   "a base is a node with one sweep, and zero with TILES sweeps")
        return bass.ds(first, P)

    def sage(msg, sums, rts, wl, last, gathered):
        S = S2
        per_store = 48 if last else 32
        pagg = psum[0:2]
        with nc.Block() as block:
            @block.gpsimd
            def _(pool):
                def body(R, j, ahead):
                    wait_here(pool, S["idx"][j], (R + 1) * 16)
                    wait_here(pool, S["rows_used"][j], R + 1)
                    for k in range(CHUNKS):
                        pool.indirect_dma_start(
                            out=G[:, j, k, 0:D], out_offset=None, in_=msg[0:NODES, :],
                            in_offset=bass.IndirectOffsetOnAxis(ap=idx[:, j, k:k + 1], axis=0)
                        ).then_inc(gathered[j], 16)
                each_step(pool, sage_rounds(pool), 2, body)

            @block.sync
            def _(sp):
                def load_idx(g, j):
                    sp.dma_start(idx[:, j, :], src_g[bass.ds(g, 1), :, :].rearrange("a p k -> (a p) k")
                                 ).then_inc(S["idx"][j], 16)

                def load_dst(g, j):
                    sp.dma_start(dst[:, j, :], dst_g[bass.ds(g, 1), :, :].rearrange("a p k -> (a p) k")
                                 ).then_inc(S["dst"][j], 16)

                def load_root(rows, j):
                    sp.dma_start(root[:, j, :], rts[rows, :]).then_inc(S["root"][j], 16)
                    if last:
                        sp.dma_start(xw[:, j, :], x[rows, :]).then_inc(S["root"][j], 16)

                for j in range(2):
                    load_idx(j, j)
                    load_dst(j, j)
                rows0 = window(sp, 0)
                load_root(rows0, 0)
                sp.dma_start(old[:, 0, 0:D + 1], sums[rows0, :]).then_inc(S["old"][0], 16)

                def body(R, j, ahead):
                    s = sp.snap(R * 2 + j)
                    n = 1 - j
                    g = group_of(sp, s + 2)
                    sp.wait_ge(gathered[j], (R + 1) * (16 * CHUNKS))
                    load_idx(g, j)
                    sp.wait_ge(S["onehot"][j], R + 1)
                    load_dst(g, j)
                    if not ahead:
                        return
                    rows = window(sp, s + 1)
                    sp.wait_ge(S["o"], s + 1)
                    if last:
                        sp.wait_ge(S["x1"], s + 1)
                    load_root(rows, n)
                    sp.wait_ge(S["sums_stored"], (s + 1) * 16)
                    sp.dma_start(old[:, n, 0:D + 1], sums[rows, :]).then_inc(S["old"][n], 16)
                rounds = sage_rounds(sp)
                each_step(sp, rounds, 2, body)
                for j in range(2):
                    wait_here(sp, S["idx"][j], (rounds + 2) * 16)
                    wait_here(sp, S["dst"][j], (rounds + 2) * 16)

            @block.vector
            def _(dve):
                def one_hot(j, g, nth, rounds):
                    dve.wait_ge(S["dst"][j], rounds * 16)
                    dve.tensor_scalar(dstrel[:, j, 0:CHUNKS], dst[:, j, :], base_t[:, bass.ds(g, 1)], None,
                                      ALU.subtract).then_inc(S["rel"], 1)
                    dve.wait_ge(S["rel"], nth)
                    dve.tensor_tensor(OH[:, j, 0:CHUNKS, :],
                                      dstrel[:, j, 0:CHUNKS].unsqueeze(2).to_broadcast([P, CHUNKS, P]),
                                      iota_row[:, :].unsqueeze(1).to_broadcast([P, CHUNKS, P]),
                                      ALU.is_equal).then_inc(S["onehot"][j], 1)
                    dve.tensor_scalar(base_t[:, bass.ds(g, 1)], base_t[:, bass.ds(g, 1)], float(P), None,
                                      ALU.add).then_inc(S["moved"], 1)
                    wait_here(dve, S["moved"], nth)

                dve.memset(G[:, 0:2, 0:CHUNKS, D:D + 1], 1.0).then_inc(S["start"], 1)
                dve.tensor_copy(base_t[:, :], base0_t[:, :]).then_inc(S["start"], 1)
                dve.wait_ge(S["start"], 2)
                for j in range(2):
                    one_hot(j, j, j + 1, 1)

                def body(R, j, ahead):
                    s = dve.snap(R * 2 + j)
                    done = dve.snap(s + 1)
                    dve.wait_ge(S["old"][j], (R + 1) * 16)
                    dve.wait_ge(S["rows_used"][j], R + 2)
                    dve.tensor_tensor(new[:, 0:D + 1], pagg[j][:, 0:D + 1], old[:, j, 0:D + 1],
                                      ALU.add).then_inc(S["merged"], 1)
                    dve.wait_ge(S["merged"], done)
                    dve.tensor_scalar(cnt[:, 0:1], new[:, D:D + 1], 1.0, None, ALU.max).then_inc(S["clip"], 1)
                    dve.wait_ge(S["clip"], done)
                    dve.reciprocal(cnt[:, 1:2], cnt[:, 0:1]).then_inc(S["rcount"], 1)
                    dve.wait_ge(S["rcount"], done)
                    dve.tensor_scalar(aggr[:, :], new[:, 0:D], cnt[:, 1:2], None, ALU.mult).then_inc(S["mean"], 1)
                    if ahead:
                        one_hot(j, group_of(dve, s + 2), dve.snap(s + 3), R + 2)
                    dve.wait_ge(S["lin"], done)
                    dve.wait_ge(S["root"][j], (R + 1) * (32 if last else 16))
                    dve.tensor_tensor(o[:, :], po[:, 0:D], root[:, j, :], ALU.add).then_inc(S["o"], 1)
                    dve.wait_ge(S["norm"], done)
                    dve.tensor_scalar(nrm[:, 2:3], nrm[:, 1:2], EPS_NORM, None, ALU.max).then_inc(S["norm_clip"], 1)
                    dve.wait_ge(S["norm_clip"], done)
                    dve.reciprocal(nrm[:, 3:4], nrm[:, 2:3]).then_inc(S["rnorm"], 1)
                    dve.wait_ge(S["stored"], done * per_store)
                    if last:
                        dve.wait_ge(S["rnorm"], done)
                        dve.scalar_tensor_tensor(out=x1n[:, :], in0=o[:, :], scalar=nrm[:, 3:4], in1=xw[:, j, :],
                                                 op0=ALU.mult, op1=ALU.add).then_inc(S["x1"], 1)
                        dve.wait_ge(S["x1"], done)
                        layer_norm_dve(dve, S, done, x1n[:, :])
                    else:
                        add_bias(dve, S, done, b2)
                each_step(dve, sage_rounds(dve), 2, body)

            @block.scalar
            def _(act):
                act.sem_inc(S["stored"], per_store)

                def body(R, j, ahead):
                    s = act.snap(R * 2 + j)
                    done = act.snap(s + 1)
                    rows = window(act, s)
                    act.wait_ge(S["merged"], done)
                    act.dma_start(sums[rows, :], new[:, 0:D + 1]).then_inc(S["sums_stored"], 16)
                    act.wait_ge(S["mean_transposed"], done)
                    act.copy(aT[:, :, :].rearrange("p c n -> p (c n)"), tpA[:, 0:D]).then_inc(S["meanT"], 1)
                    act.wait_ge(S["o"], done)
                    act.activation(junk[:, :], o[:, :], ACT.Square, accum_out=nrm[:, 0:1]).then_inc(S["squares"], 1)
                    act.wait_ge(S["squares"], done)
                    act.activation(nrm[:, 1:2], nrm[:, 0:1], ACT.Sqrt).then_inc(S["norm"], 1)
                    if last:
                        layer_norm_act(act, S, done, x1n[:, :])
                        copy_hT(act, S, done)
                        act.wait_ge(S["projected"], done)
                        act.wait_ge(S["stored"], done * per_store)
                        act.copy(y[:, 0:D + 2 * HEADS], py[:, 0:D + 2 * HEADS]).then_inc(S["feats"], 1)
                        act.wait_ge(S["feats"], done)
                        act.dma_start(msg3[rows, :], y[:, 0:D + HEADS]).then_inc(S["stored"], 16)
                        act.dma_start(self3[rows, :], y[:, D + HEADS:D + 2 * HEADS]).then_inc(S["stored"], 16)
                        act.dma_start(x1[rows, :], x1n[:, :]).then_inc(S["stored"], 16)
                    else:
                        act.wait_ge(S["rnorm"], done)
                        act.activation(h[:, :], o[:, :], ACT.Relu, scale=nrm[:, 3:4]).then_inc(S["h"], 1)
                        copy_hT(act, S, done)
                        relu_and_store(act, S, done, msg2[rows, :], root2[rows, :])
                rounds = sage_rounds(act)
                each_step(act, rounds, 2, body)
                steps = act.snap(rounds * 2 + 2)
                wait_here(act, S["stored"], (steps + 1) * per_store)
                wait_here(act, S["sums_stored"], steps * 16)

            @block.tensor
            def _(pe):
                for j in range(2):
                    pe.sem_inc(S["rows_used"][j], 1)

                def sum_rows(j, chunks):
                    for k in chunks:
                        ins = pe.matmul(pagg[j][:, 0:D + 1], OH[:, j, k, :], G[:, j, k, 0:D + 1], start=(k == 0),
                                        stop=(k == CHUNKS - 1))
                        if k == CHUNKS - 1:
                            ins.then_inc(S["rows_used"][j], 1)

                pe.wait_ge(S["onehot"][0], 1)
                pe.wait_ge(gathered[0], 16 * CHUNKS)
                sum_rows(0, range(CHUNKS))

                def body(R, j, ahead):
                    done = pe.snap(R * 2 + (j + 1))
                    n = 1 - j
                    if ahead:
                        pe.wait_ge(S["onehot"][n], R + (1 + j))
                        pe.wait_ge(gathered[n], (R + (1 + j)) * (16 * CHUNKS))
                        sum_rows(n, range(0, 3))
                    pe.wait_ge(S["mean"], done)
                    for c in range(2):
                        ins = pe.transpose(tpA[:, c * P:(c + 1) * P], aggr[:, c * P:(c + 1) * P], ident[:, :])
                    ins.then_inc(S["mean_transposed"], 1)
                    if ahead:
                        sum_rows(n, range(3, 5))
                    pe.wait_ge(S["meanT"], done)
                    for c in range(2):
                        ins = pe.matmul(po[:, 0:D], aT[:, c, :], wl[:, c, :], start=(c == 0), stop=(c == 1))
                    ins.then_inc(S["lin"], 1)
                    if ahead:
                        sum_rows(n, range(5, 10))
                    transpose_h(pe, S, done)
                    if ahead:
                        sum_rows(n, range(10, CHUNKS))
                    project(pe, S, done, wg if last else wpr2, D + 2 * HEADS if last else 2 * D)
                each_step(pe, sage_rounds(pe), 2, body)

    def clear(S):
        for sem in S.values():
            for one in (sem if isinstance(sem, list) else [sem]):
                nc.sync.sem_clear(one)
        nc.all_engine_barrier()

    sage(msg1, sum1, root1, wl1, False, G1["rows"])
    clear(S2)
    sage(msg2, sum2, root2, wl2, True, G2["rows"])
    finish(S2)

    recs = sb("recs", [P, RING, ACHUNKS, 4], i32)
    own = sb("own", [P, RING, HEADS])
    top = sb("top", [P, RING, HEADS])
    OT = sb("OT", [P, 2, ACHUNKS, P], bf16)
    own3, own_r = sb("own3", [P, 3, HEADS], bf16), sb("own_r", [P, HEADS])
    z = sb("z", [P, 2, ACHUNKS, HEADS])
    E, Er = sb("E", [P, 2, ACHUNKS, HEADS]), sb("Er", [P, ACHUNKS * HEADS])
    mixed = sb("mixed", [P, ACHUNKS // PART, MIXED], bf16)
    mixedT = sb("mixedT", [MIXED, 2, ACHUNKS // PART, P], bf16)
    cmax = sb("cmax", [P, ACHUNKS, HEADS])
    gmax, tmax = sb("gmax", [P, HEADS]), sb("tmax", [P, HEADS])
    max3, max_r = sb("max3", [P, 3, HEADS], bf16), sb("max_r", [P, HEADS])
    fade_by, fade = sb("fade_by", [P, 2, HEADS]), sb("fade", [P, 2, HEADS])
    zd = sb("zd", [P, 2, ACHUNKS, HEADS])
    pr = sb("pr", [P, ACHUNKS, HEADS])
    faded = sb("faded", [P, D + HEADS])
    rden = sb("rden", [P, 2, HEADS])
    outw = sb("outw", [P, 3, D])
    NS = ACHUNKS * HEADS
    parts = "p (k i h) -> p k h i"
    by_head = "p (h o) -> p h o"
    OT_SETS = [range(a, min(a + 4, ACHUNKS)) for a in range(0, ACHUNKS, 4)]
    BY_ACT = ACHUNKS - BY_DVE
    SUM_ORDER = list(range(BY_ACT, ACHUNKS)) + list(range(BY_ACT))
    SUMS_NOW = 12
    SCALED_FIRST = 10
    pown, pedge, pOT, pbc, pagg = psum[0][:, 0:3 * NS], psum[0][:, 256:256 + 3 * NS], psum[2:4], psum[4:7], psum[7]
    pmixed = psum[1][0:MIXED, 0:ACHUNKS // PART * P // 2].bitcast(bf16)
    S3 = semaphores("gat", ["OT_out", "OT", "masks", "own_hi", "own_r", "own_mid", "own3", "z_own", "z_sum", "z", "leaky",
                            "E", "E_hi", "E_r", "E_mid", "E3", "mixed_out", "mixedT", "spread", "chunk_max", "gmax",
                            "tmax", "max_hi", "max_r", "max_mid", "max3", "fade_by", "fade", "m_edge", "m_sum", "below",
                            "clipped", "p", "p_den", "V_act", "V_dve", "keep", "merged", "den", "rden", "mean",
                            "biased", "out", "out_stored", "att_stored", "top_stored"],
                    ["rec", "rows_used", "onehot", "own", "top", "old"], RING)
    rows3 = G3["rows"]

    def rounds3(e):
        return e.value_load(rounds_i[0:1, 0:1], min_val=1, max_val=MOST_ROUNDS - 1)

    def window3(e, step):
        return bass.ds(e.value_load(base3_i[0:1, bass.ds(step, 1)], min_val=0, max_val=TILES * P), P)

    def kept(e, value):
        return value if isinstance(value, int) else e.snap(value)

    def uses(R, m):
        return R + (m // RING + 1)

    def all_steps(e, rounds, body):
        body(0, 0, True, True)
        with e.Fori(0, rounds) as R:
            for m in range(1, RING + 1):
                body(R, m, True, True)
        for m in range(1, RING + 1):
            body(rounds, m, m + 2 <= RING, m + 1 <= RING)

    with nc.Block() as block:
        @block.gpsimd
        def _(pool):
            def gather(R, j):
                wait_here(pool, S3["rec"][j], (R + 1) * 16)
                wait_here(pool, S3["rows_used"][j], R + 1)
                for k in range(ACHUNKS):
                    pool.indirect_dma_start(
                        out=G[:, j, k, 0:D + HEADS], out_offset=None, in_=msg3[0:NODES, :],
                        in_offset=bass.IndirectOffsetOnAxis(ap=recs[:, j, k, 0:1], axis=0)
                    ).then_inc(rows3[j], 16)
            gather(0, 0)
            with pool.Fori(0, rounds3(pool) + 1) as R:
                for m in range(1, RING + 1):
                    gather(kept(pool, R + m // RING), m % RING)

        @block.sync
        def _(sp):
            records = rec_d.rearrange("(s p k) c -> s p (k c)", p=P, k=ACHUNKS)

            def load_rec(s, j):
                sp.dma_start(recs[:, j, :, :].rearrange("p k c -> p (k c)"),
                             records[bass.ds(s, 1), :, :].rearrange("a p k -> (a p) k")).then_inc(S3["rec"][j], 16)

            def load_own(rows, j):
                sp.dma_start(own[:, j, :], self3[rows, :]).then_inc(S3["own"][j], 16)

            def load_top_and_x(rows, j):
                sp.dma_start(top[:, j, :], att3[rows, D + HEADS:D + 2 * HEADS]).then_inc(S3["top"][j], 16)
                sp.dma_start(xw[:, j, :], x1[rows, :]).then_inc(S3["old"][j], 16)

            for j in range(RING):
                load_rec(j, j)
            for j in range(3):
                load_own(window3(sp, j), j)
            load_top_and_x(window3(sp, 0), 0)

            def finish_last(rows, done):
                wait_here(sp, S3["merged"], done)
                sp.dma_start(att3[rows, 0:D + HEADS], new[:, 0:D + HEADS]).then_inc(S3["att_stored"], 16)

            def store_out(rows, done):
                wait_here(sp, S3["out"], done)
                sp.dma_start(out[rows, :], outw[:, 2, :]).then_inc(S3["out_stored"], 16)

            def body(R, m, scores, largest):
                s = kept(sp, R * RING + m)
                j, n1, n3 = m % RING, (m + 1) % RING, (m + 3) % RING
                rows, rows1, rows3_ = window3(sp, s), window3(sp, kept(sp, s + 1)), window3(sp, kept(sp, s + 3))
                rows_before = window3(sp, kept(sp, s + (-1))) if m else None
                s4 = kept(sp, s + 4)
                wait_here(sp, S3["tmax"], kept(sp, s + 1))
                sp.dma_start(att3[rows, D + HEADS:D + 2 * HEADS], tmax[:, :]).then_inc(S3["top_stored"], 16)
                load_own(rows3_, n3)
                wait_here(sp, rows3[j], kept(sp, uses(R, m) * (16 * ACHUNKS)))
                load_rec(s4, j)
                wait_here(sp, S3["top_stored"], kept(sp, (s + 1) * 16))
                if largest:
                    load_top_and_x(rows1, n1)
                if m:
                    finish_last(rows_before, s)
                    wait_here(sp, S3["att_stored"], kept(sp, s * 16))
                sp.dma_start(old[:, j, 0:D + HEADS], att3[rows, 0:D + HEADS]).then_inc(S3["old"][j], 16)
                if m:
                    store_out(rows_before, s)
            rounds = rounds3(sp)
            all_steps(sp, rounds, body)
            steps = kept(sp, rounds * RING + (RING + 1))
            last = window3(sp, kept(sp, rounds * RING + RING))
            finish_last(last, steps)
            store_out(last, steps)
            wait_here(sp, S3["att_stored"], kept(sp, steps * 16))
            wait_here(sp, S3["out_stored"], kept(sp, steps * 16 + 16))
            for j in range(RING):
                wait_here(sp, S3["rec"][j], kept(sp, (rounds + (3 if j == 0 else 2)) * 16))
                wait_here(sp, S3["own"][j], kept(sp, (rounds + 2) * 16))

        @block.vector
        def _(dve):
            def high_part(three, src, sem):
                dve.tensor_copy(three(0), src).then_inc(sem, 1)

            def what_is_left(rest, src, three, sem):
                dve.tensor_tensor(rest, src, three(0), ALU.subtract).then_inc(sem, 1)

            def middle_part(three, rest, sem):
                dve.tensor_copy(three(1), rest).then_inc(sem, 1)

            def low_part(three, rest, sem):
                dve.tensor_tensor(three(2), rest, three(1), ALU.subtract).then_inc(sem, 1)

            def own_three(q):
                return own3[:, q, :]

            def max_three(q):
                return max3[:, q, :]

            def E_three(q):
                return mixed[:, :, q * PQ:(q + 1) * PQ]

            def E_flat(b):
                return E[:, b, :, :].rearrange("p k h -> p (k h)").rearrange("p (a q) -> p a q", q=PQ)

            E_rest = Er[:, :].rearrange("p (a q) -> p a q", q=PQ)

            def one_hot(n, Rn):
                dve.wait_ge(S3["rec"][n], kept(dve, Rn * 16))
                dve.tensor_tensor(OH[:, n, :, :],
                                  recs[:, n, :, 1:2].bitcast(f32).to_broadcast([P, ACHUNKS, P]),
                                  iota_row[:, :].unsqueeze(1).to_broadcast([P, ACHUNKS, P]),
                                  ALU.is_equal).then_inc(S3["onehot"][n], 1)

            def masks(n, done):
                for at, width, digit in ((0, HI, 1), (HI, LO, 0)):
                    to = mixed[:, :, SCORES:].rearrange("p a (c r) -> p a c r", c=PART)[:, :, :, at:at + width]
                    of = recs[:, n, :, 3:4].bitcast(bf16)[:, :, digit:digit + 1].rearrange(
                        "p (a c) o -> p a c o", c=PART).to_broadcast([P, ACHUNKS // PART, PART, width])
                    by = iota_b[:, 0:width].unsqueeze(1).unsqueeze(1).to_broadcast(
                        [P, ACHUNKS // PART, PART, width])
                    ins = dve.tensor_tensor(to, of, by, ALU.not_equal)
                ins.then_inc(S3["masks"], 1)

            def z_sum(done):
                dve.wait_ge(S3["z_own"], done)
                dve.tensor_reduce(z[:, 0, :, :], pown[:, 0:3 * NS].rearrange(parts, i=3, h=HEADS), axis=AX.X,
                                  op=ALU.add).then_inc(S3["z_sum"], 1)

            def z_add(n, Rn, done):
                dve.wait_ge(rows3[n], kept(dve, Rn * (16 * ACHUNKS)))
                dve.wait_ge(S3["z_sum"], done)
                dve.tensor_tensor(z[:, 1, :, :], z[:, 0, :, :], G[:, n, :, D:D + HEADS], ALU.add).then_inc(S3["z"], 1)

            def leaky(done):
                dve.wait_ge(S3["z"], done)
                dve.scalar_tensor_tensor(out=z[:, 0, :, :], in0=z[:, 1, :, :], scalar=0.2, in1=z[:, 1, :, :],
                                         op0=ALU.mult, op1=ALU.max).then_inc(S3["leaky"], 1)

            def weigh(n, b, done):
                dve.wait_ge(S3["leaky"], done)
                dve.tensor_tensor(E[:, b, :, :], z[:, 0, :, :],
                                  recs[:, n, :, 2:3].bitcast(f32).to_broadcast([P, ACHUNKS, HEADS]),
                                  ALU.mult).then_inc(S3["E"], 1)

            def largest_of(first, k):
                dve.wait_ge(S3["spread"], kept(dve, first + (k + 1)))
                dve.tensor_reduce(cmax[:, k, :], pbc[k % 3][:, :].rearrange("p (h e) -> p h e", h=HEADS),
                                  axis=AX.X, op=ALU.max).then_inc(S3["chunk_max"], 1)

            def largest_in_group(first):
                dve.wait_ge(S3["chunk_max"], kept(dve, first + ACHUNKS))
                dve.tensor_reduce(gmax[:, :], cmax[:, :, :].rearrange("p k h -> p h k"), axis=AX.X,
                                  op=ALU.max).then_inc(S3["gmax"], 1)

            def merge(j, Rj, done):
                dve.wait_ge(S3["keep"], done)
                dve.wait_ge(S3["rows_used"][j], Rj)
                dve.tensor_tensor(new[:, 0:D + HEADS], pagg[:, 0:D + HEADS], faded[:, :], ALU.add
                                  ).then_inc(S3["merged"], 1)

            def keep(b, j, Rj, done):
                dve.wait_ge(S3["fade"], done)
                dve.wait_ge(S3["old"][j], kept(dve, Rj * 32))
                dve.tensor_tensor(faded[:, 0:D].rearrange(by_head, h=HEADS),
                                  old[:, j, 0:D].rearrange(by_head, h=HEADS),
                                  fade[:, b, :].unsqueeze(2).to_broadcast([P, HEADS, HD]), ALU.mult)
                dve.tensor_tensor(faded[:, D:], old[:, j, D:D + HEADS], fade[:, b, :], ALU.mult
                                  ).then_inc(S3["keep"], 1)

            def denominators(done):
                dve.wait_ge(S3["merged"], done)
                dve.tensor_scalar(rden[:, 0, :], new[:, D:D + HEADS], 1e-30, None, ALU.max).then_inc(S3["den"], 1)

            def reciprocals(done):
                dve.wait_ge(S3["den"], done)
                dve.reciprocal(rden[:, 1, :], rden[:, 0, :]).then_inc(S3["rden"], 1)

            def mean(done):
                dve.wait_ge(S3["rden"], done)
                dve.tensor_tensor(outw[:, 0, :].rearrange(by_head, h=HEADS), new[:, 0:D].rearrange(by_head, h=HEADS),
                                  rden[:, 1, :].unsqueeze(2).to_broadcast([P, HEADS, HD]), ALU.mult
                                  ).then_inc(S3["mean"], 1)

            def add_bias3(done):
                dve.wait_ge(S3["mean"], done)
                dve.tensor_tensor(outw[:, 1, :], outw[:, 0, :], bias_t[:, :], ALU.add).then_inc(S3["biased"], 1)

            def output(j, done):
                dve.wait_ge(S3["biased"], done)
                dve.wait_ge(S3["out_stored"], kept(dve, done * 16))
                dve.scalar_tensor_tensor(out=outw[:, 2, :], in0=outw[:, 1, :], scalar=0.0, in1=xw[:, j, :],
                                         op0=ALU.max, op1=ALU.add).then_inc(S3["out"], 1)

            for t in range(3):
                one_hot(t, 1)
            for t in range(2):
                dve.wait_ge(S3["own"][t], 16)
                high_part(own_three, own[:, t, :], S3["own_hi"])
                dve.wait_ge(S3["own_hi"], t + 1)
                what_is_left(own_r[:, :], own[:, t, :], own_three, S3["own_r"])
                dve.wait_ge(S3["own_r"], t + 1)
                middle_part(own_three, own_r[:, :], S3["own_mid"])
                dve.wait_ge(S3["own_mid"], t + 1)
                low_part(own_three, own_r[:, :], S3["own3"])
                if t:
                    dve.wait_ge(S3["mixed_out"], t)
                masks(t, t + 1)
                z_sum(t + 1)
                z_add(t, 1, t + 1)
                leaky(t + 1)
                weigh(t, t, t + 1)
                dve.wait_ge(S3["E"], t + 1)
                high_part(E_three, E_flat(t), S3["E_hi"])
                dve.wait_ge(S3["E_hi"], t + 1)
                what_is_left(E_rest, E_flat(t), E_three, S3["E_r"])
                dve.wait_ge(S3["E_r"], t + 1)
                middle_part(E_three, E_rest, S3["E_mid"])
                dve.wait_ge(S3["E_mid"], t + 1)
                low_part(E_three, E_rest, S3["E3"])
            for k in range(ACHUNKS):
                largest_of(0, k)
            largest_in_group(0)

            def body(R, m, scores, largest):
                s = kept(dve, R * RING + m)
                done, done1, done3 = kept(dve, s + 1), kept(dve, s + 2), kept(dve, s + 3)
                j, before, n2, n3 = m % RING, (m + 3) % RING, (m + 2) % RING, (m + 3) % RING
                b, b1 = m % 2, (m + 1) % 2
                first = kept(dve, done * ACHUNKS)
                U, U2, U3 = uses(R, m), uses(R, m + 2), uses(R, m + 3)
                Ub = uses(R, m - 1)
                dve.wait_ge(S3["gmax"], done)
                dve.wait_ge(S3["top"][j], kept(dve, U * 16))
                dve.tensor_tensor(tmax[:, :], top[:, j, :], gmax[:, :], ALU.max).then_inc(S3["tmax"], 1)
                if largest:
                    largest_of(first, 0)
                dve.wait_ge(S3["tmax"], done)
                high_part(max_three, tmax[:, :], S3["max_hi"])
                if largest:
                    largest_of(first, 1)
                dve.wait_ge(S3["max_hi"], done)
                what_is_left(max_r[:, :], tmax[:, :], max_three, S3["max_r"])
                if largest:
                    largest_of(first, 2)
                dve.wait_ge(S3["max_r"], done)
                middle_part(max_three, max_r[:, :], S3["max_mid"])
                if largest:
                    largest_of(first, 3)
                dve.wait_ge(S3["max_mid"], done)
                low_part(max_three, max_r[:, :], S3["max3"])
                dve.tensor_tensor(fade_by[:, b, :], top[:, j, :], tmax[:, :], ALU.subtract).then_inc(S3["fade_by"], 1)
                if largest:
                    largest_of(first, 4)
                if m:
                    keep(b1, before, Ub, s)
                if scores:
                    dve.wait_ge(S3["own"][n2], kept(dve, U2 * 16))
                    high_part(own_three, own[:, n2, :], S3["own_hi"])
                if largest:
                    largest_of(first, 5)
                dve.wait_ge(S3["m_edge"], done)
                dve.tensor_reduce(zd[:, 0, :, :], pedge[:, 0:3 * NS].rearrange(parts, i=3, h=HEADS), axis=AX.X,
                                  op=ALU.add).then_inc(S3["m_sum"], 1)
                if scores:
                    dve.wait_ge(S3["own_hi"], done3)
                    what_is_left(own_r[:, :], own[:, n2, :], own_three, S3["own_r"])
                if largest:
                    largest_of(first, 6)
                dve.wait_ge(S3["m_sum"], done)
                dve.tensor_tensor(zd[:, 1, :, :], E[:, b, :, :], zd[:, 0, :, :], ALU.subtract).then_inc(S3["below"], 1)
                if scores:
                    dve.wait_ge(S3["own_r"], done3)
                    middle_part(own_three, own_r[:, :], S3["own_mid"])
                if largest:
                    largest_of(first, 7)
                dve.wait_ge(S3["below"], done)
                dve.tensor_scalar(zd[:, 0, :, :], zd[:, 1, :, :], 0.0, None, ALU.min).then_inc(S3["clipped"], 1)
                if scores:
                    dve.wait_ge(S3["own_mid"], done3)
                    low_part(own_three, own_r[:, :], S3["own3"])
                if largest:
                    largest_of(first, 8)
                if m:
                    merge(before, kept(dve, Ub + 1), s)
                dve.wait_ge(S3["p"], done)
                dve.tensor_tensor(G[:, j, BY_ACT:, 0:D].rearrange("p k (h o) -> p k h o", h=HEADS),
                                  G[:, j, BY_ACT:, 0:D].rearrange("p k (h o) -> p k h o", h=HEADS),
                                  pr[:, BY_ACT:, :].unsqueeze(3).to_broadcast([P, BY_DVE, HEADS, HD]),
                                  ALU.mult).then_inc(S3["V_dve"], 1)
                if largest:
                    largest_of(first, 9)
                if m:
                    denominators(s)
                if scores:
                    dve.wait_ge(S3["mixed_out"], done1)
                    masks(n2, done3)
                if largest:
                    largest_of(first, 10)
                if m:
                    reciprocals(s)
                if scores:
                    z_sum(done3)
                if largest:
                    largest_of(first, 11)
                if m:
                    mean(s)
                if scores:
                    z_add(n2, U2, done3)
                if largest:
                    largest_of(first, 12)
                if m:
                    add_bias3(s)
                if scores:
                    leaky(done3)
                if largest:
                    largest_of(first, 13)
                if m:
                    output(before, s)
                if scores:
                    weigh(n2, b, done3)
                if largest:
                    largest_of(first, 14)
                if scores:
                    dve.wait_ge(S3["E"], done3)
                    high_part(E_three, E_flat(b), S3["E_hi"])
                if largest:
                    largest_of(first, 15)
                if scores:
                    dve.wait_ge(S3["E_hi"], done3)
                    what_is_left(E_rest, E_flat(b), E_three, S3["E_r"])
                if largest:
                    largest_of(first, 16)
                if scores:
                    dve.wait_ge(S3["E_r"], done3)
                    middle_part(E_three, E_rest, S3["E_mid"])
                if largest:
                    largest_of(first, 17)
                if scores:
                    dve.wait_ge(S3["E_mid"], done3)
                    low_part(E_three, E_rest, S3["E3"])
                if largest:
                    largest_in_group(first)
                if scores:
                    one_hot(n3, U3)
            rounds = rounds3(dve)
            dve.sem_inc(S3["out_stored"], 16)
            all_steps(dve, rounds, body)
            steps = kept(dve, rounds * RING + (RING + 1))
            keep(0, 0, kept(dve, rounds + 2), steps)
            merge(0, kept(dve, rounds + 3), steps)
            denominators(steps)
            reciprocals(steps)
            mean(steps)
            add_bias3(steps)
            output(0, steps)

        @block.scalar
        def _(act):
            def copy_OT(before, a, b):
                chunks = OT_SETS[a]
                act.wait_ge(S3["OT_out"], kept(act, before + (a + 1)))
                act.copy(OT[:, b, chunks[0]:chunks[-1] + 1, :].rearrange("p k n -> p (k n)"),
                         pOT[a % 2][:, 0:len(chunks) * P]).then_inc(S3["OT"], 1)

            def copy_mixed(b, done):
                act.wait_ge(S3["mixed_out"], done)
                act.copy(mixedT[:, b, :, :].rearrange("p a n -> p (a n)"), pmixed).then_inc(S3["mixedT"], 1)

            def scale(j, chunks):
                for k in chunks:
                    for q in range(HEADS):
                        row = G[:, j, k, q * HD:(q + 1) * HD]
                        ins = act.activation(row, row, ACT.Copy, scale=pr[:, k, q:q + 1])
                    ins.then_inc(S3["V_act"], 1)

            for t in range(2):
                for a in range(len(OT_SETS)):
                    copy_OT(t * len(OT_SETS), a, t)
                copy_mixed(t, t + 1)

            def body(R, m, scores, largest):
                s = kept(act, R * RING + m)
                done = kept(act, s + 1)
                j, b = m % RING, m % 2
                sets = kept(act, (s + 2) * len(OT_SETS))
                act.wait_ge(S3["fade_by"], done)
                act.activation(fade[:, b, :], fade_by[:, b, :], ACT.Exp).then_inc(S3["fade"], 1)
                if scores:
                    for a in range(2):
                        copy_OT(sets, a, b)
                act.wait_ge(S3["clipped"], done)
                if m:
                    act.wait_ge(S3["V_act"], kept(act, s * BY_ACT))
                act.activation(pr[:, :, :], zd[:, 0, :, :], ACT.Exp).then_inc(S3["p"], 1)
                act.wait_ge(S3["p"], done)
                act.copy(G[:, j, :, D:D + HEADS], pr[:, :, :]).then_inc(S3["p_den"], 1)
                if scores:
                    for a in range(2, len(OT_SETS)):
                        copy_OT(sets, a, b)
                scale(j, range(0, SCALED_FIRST))
                if scores:
                    copy_mixed(b, kept(act, s + 3))
                scale(j, range(SCALED_FIRST, BY_ACT))
            all_steps(act, rounds3(act), body)

        @block.tensor
        def _(pe):
            for j in range(RING):
                pe.sem_inc(S3["rows_used"][j], 1)

            def exchange(n, before, a):
                if a >= 2:
                    pe.wait_ge(S3["OT"], kept(pe, before + (a - 1)))
                for c, k in enumerate(OT_SETS[a]):
                    ins = pe.transpose(pOT[a % 2][:, c * P:(c + 1) * P], OH[:, n, k, :], ident[:, :])
                ins.then_inc(S3["OT_out"], 1)

            def own_scores(b, before, done):
                pe.wait_ge(S3["own3"], done)
                pe.wait_ge(S3["OT"], kept(pe, before + len(OT_SETS)))
                for k in range(ACHUNKS):
                    ins = pe.matmul(pown[:, k * 3 * HEADS:(k + 1) * 3 * HEADS], OT[:, b, k, :],
                                    own3[:, :, :].rearrange("p i h -> p (i h)"), start=True, stop=True)
                ins.then_inc(S3["z_own"], 1)

            def exchange_scores(done):
                pe.wait_ge(S3["masks"], done)
                pe.wait_ge(S3["E3"], done)
                for a in range(ACHUNKS // PART):
                    ins = pe.transpose(pmixed[:, a * P:(a + 1) * P], mixed[:, a, :], identb[:, :])
                ins.then_inc(S3["mixed_out"], 1)

            def spread(b, first, k):
                bank = pbc[k % 3]
                if k >= 3 or not isinstance(first, int) or first:
                    pe.wait_ge(S3["chunk_max"], kept(pe, first + (k - 2)))
                for q in range(HEADS):
                    ins = pe.matmul(bank[:, q * P:(q + 1) * P], sel[:, (k % PART) * HEADS + q, :],
                                    mixedT[:, b, k // PART, :], start=True, stop=True)
                ins.then_inc(S3["spread"], 1)

            def sum_rows(s, done, j, q):
                k = SUM_ORDER[q]
                if q == 0:
                    pe.wait_ge(S3["p_den"], done)
                    pe.wait_ge(S3["V_dve"], done)
                if k < BY_ACT:
                    pe.wait_ge(S3["V_act"], kept(pe, s * BY_ACT + (k + 1)))
                ins = pe.matmul(pagg[:, 0:D + HEADS], OH[:, j, k, :], G[:, j, k, 0:D + HEADS], start=(q == 0),
                                stop=(q == ACHUNKS - 1))
                if q == ACHUNKS - 1:
                    ins.then_inc(S3["rows_used"][j], 1)

            for t in range(2):
                pe.wait_ge(S3["onehot"][t], 1)
                for a in range(len(OT_SETS)):
                    exchange(t, t * len(OT_SETS), a)
                own_scores(t, t * len(OT_SETS), t + 1)
                if t:
                    pe.wait_ge(S3["mixedT"], t)
                exchange_scores(t + 1)
            pe.wait_ge(S3["mixedT"], 1)
            for k in range(ACHUNKS):
                spread(0, 0, k)

            def body(R, m, scores, largest):
                s = kept(pe, R * RING + m)
                done, done3 = kept(pe, s + 1), kept(pe, s + 3)
                j, before, n2 = m % RING, (m + 3) % RING, (m + 2) % RING
                b, b1 = m % 2, (m + 1) % 2
                first = kept(pe, done * ACHUNKS)
                sets = kept(pe, (s + 2) * len(OT_SETS))
                if largest:
                    pe.wait_ge(S3["mixedT"], kept(pe, s + 2))
                left = list(range(SUMS_NOW, ACHUNKS))
                now = list(range(SUMS_NOW))
                for k in range(ACHUNKS):
                    if largest:
                        spread(b1, first, k)
                    if m and left:
                        sum_rows(kept(pe, s + (-1)), s, before, left.pop(0))
                    if k == 6:
                        pe.wait_ge(S3["max3"], done)
                        for c in range(ACHUNKS):
                            ins = pe.matmul(pedge[:, c * 3 * HEADS:(c + 1) * 3 * HEADS], OT[:, b, c, :],
                                            max3[:, :, :].rearrange("p i h -> p (i h)"), start=True, stop=True)
                        ins.then_inc(S3["m_edge"], 1)
                        if scores:
                            pe.wait_ge(S3["onehot"][n2], uses(R, m + 2))
                            for a in range(2):
                                exchange(n2, sets, a)
                    if k in (7, 8, 9) and scores:
                        exchange(n2, sets, k - 5)
                    if k == 9 and scores:
                        own_scores(b, sets, done3)
                    if k >= 11:
                        if k == 11 and m:
                            pe.wait_ge(S3["merged"], s)
                        for q in range(2):
                            if now:
                                sum_rows(s, done, j, now.pop(0))
                while now:
                    sum_rows(s, done, j, now.pop(0))
                if scores:
                    exchange_scores(done3)
            rounds = rounds3(pe)
            all_steps(pe, rounds, body)
            for q in range(SUMS_NOW, ACHUNKS):
                sum_rows(kept(pe, rounds * RING + RING), kept(pe, rounds * RING + (RING + 1)), 0, q)


def kernel(**inputs):
    import numpy as np
    import concourse.bacc as bacc
    from concourse.bass_utils import run_bass_kernel_spmd

    def filled(a, fill):
        a = np.asarray(a)
        return np.concatenate([a, np.full(ALL * P - EDGES, fill, a.dtype)])

    def by_partition(a, blocks, chunks):
        return np.ascontiguousarray(a.reshape(blocks, chunks, P).transpose(0, 2, 1))

    def by_block(a):
        a = a.reshape(2, BLOCKS, BC, P).transpose(1, 3, 0, 2).reshape(BLOCKS, P, 2 * BC)
        return np.concatenate([a, np.zeros_like(a[:2])])

    src, dst, weight = inputs["src"], inputs["dst"], inputs["edge_weight"]
    dst_filled = filled(dst, NO_NODE)
    arrays = {"x": np.concatenate([np.asarray(inputs["x"]), np.zeros((ROWS + 2 * P - NODES, D), np.float32)]),
              "src_g": by_partition(filled(src, 0), GROUPS, CHUNKS), "dst_g": by_partition(dst_filled, GROUPS, CHUNKS),
              "dst_s": dst_filled.reshape(GROUPS, GE), "src_p": filled(src, PAD_SRC).reshape(P, ALL),
              "src_b": by_block(filled(src, PAD_SRC)), "dst_b": by_block(filled(dst, 0)),
              "w_b": by_block(filled(weight, 0))}
    for name in ("W_proj1", "b_proj1", "W_l1", "b_l1", "W_r1", "W_proj2", "b_proj2", "W_l2", "b_l2", "W_r2"):
        arrays[name] = np.ascontiguousarray(inputs[f"L0_gnn_{name}"])
    arrays["W"] = np.ascontiguousarray(inputs["L1_gnn_W"])
    for name in ("a_self", "a_neigh", "bias"):
        arrays[name] = np.ascontiguousarray(inputs[f"L1_gnn_{name}"]).reshape(-1)
    nc = bacc.Bacc("TRN2", target_bir_lowering=False, num_devices=1)
    args = [nc.dram_tensor(f"in_{n}", a.shape, mybir.dt.from_np(a.dtype), kind="ExternalInput").ap()
            for n, a in arrays.items()]
    out = nc.dram_tensor("out", [ROWS, D], mybir.dt.float32, kind="ExternalOutput").ap()
    gnn_program(nc, *args, out)
    r = run_bass_kernel_spmd(nc, [{f"in_{n}": a for n, a in arrays.items()}], core_ids=[0])
    return r.results[0]["out"][:NODES]
```
